# Optimizing a Trainium2 kernel written in Bass

```python
import numpy as np
import jax
import jax.numpy as jnp

def _softmax(x, axis=-1):
    return jax.nn.softmax(x, axis=axis)

def _gelu(x):
    return jax.nn.gelu(x, approximate=True)

def _silu(x):
    return jax.nn.silu(x)

def _sigmoid(x):
    return jax.nn.sigmoid(x)

def _layernorm(x, axis=-1, eps=1e-05):
    m = jnp.mean(x, axis=axis, keepdims=True)
    v = jnp.var(x, axis=axis, keepdims=True)
    return (x - m) / jnp.sqrt(v + eps)

def _scatter_add(tgt, idx, src, axis=0):
    return tgt.at[idx].add(src)

def _segment_sum(src, seg, n):
    return jax.ops.segment_sum(src, seg, n)
kernel_name = 'mk_decoder_preln_d1_seqx_r4_81d2ee'

def setup_inputs(seed: int=0):
    np.random.seed(seed)
    _w = jnp.asarray

    def _rec_inputs():
        import jax
        import jax.numpy as jnp
        _rk = jax.random.key(seed)
        x = 7.22e-05 + 1 * jax.random.normal(jax.random.fold_in(_rk, 1), (4, 512, 512), jnp.float32)
        _lenS = 512 - jax.random.randint(jax.random.fold_in(_rk, 7), (4,), 0, max(1, 512 // 4) + 1, jnp.int32)
        _lenS2 = 512 - jax.random.randint(jax.random.fold_in(_rk, 8), (4,), 0, max(1, 512 // 4) + 1, jnp.int32)
        _ctx_2048P = jax.random.normal(jax.random.fold_in(_rk, 11), (4, 16, 512), jnp.float32)
        _ctx_2048c = jax.random.dirichlet(jax.random.fold_in(_rk, 511), 0.3 * jnp.ones((16,), jnp.float32), (4, 512))
        _ctx_2048t = jnp.einsum('bsk,bkd->bsd', _ctx_2048c, _ctx_2048P)
        _ctx_2048t = _ctx_2048t * jax.lax.rsqrt(jnp.mean(jnp.square(_ctx_2048t)) + 1e-12) * 0.953939
        ctx_2048 = 4.13588e-05 + 0.999923 * (_ctx_2048t + 0.3 * jax.random.normal(jax.random.fold_in(_rk, 611), (4, 512, 512), jnp.float32))
        return (x, ctx_2048)
    x, ctx_2048 = _rec_inputs()

    def _L0_attn_setup():
        import jax, jax.numpy as jnp
        import numpy as np
        B, T, H, NH = (4, 512, 512, 16)
        HD = H // NH
        SCALE = HD ** (-0.5)
        key = jax.random.key(seed)
        ks = jax.random.split(key, 9)
        s = H ** (-0.5)
        return {'x': jax.random.normal(ks[0], (B, T, H), jnp.float32), 'q_w': jax.random.normal(ks[1], (H, H), jnp.float32) * s, 'q_b': jnp.zeros((H,), jnp.float32), 'k_w': jax.random.normal(ks[2], (H, H), jnp.float32) * s, 'k_b': jnp.zeros((H,), jnp.float32), 'v_w': jax.random.normal(ks[3], (H, H), jnp.float32) * s, 'v_b': jnp.zeros((H,), jnp.float32), 'o_w': jax.random.normal(ks[4], (H, H), jnp.float32) * s, 'o_b': jnp.zeros((H,), jnp.float32)}
    _L0_attn_all = _L0_attn_setup()
    _L0_attn_in = {k: v for k, v in _L0_attn_all.items() if k in ('q_w', 'q_b', 'k_w', 'k_b', 'v_w', 'v_b', 'o_w', 'o_b')}
    del _L0_attn_all

    def _L0_xattn_setup():
        import math
        import jax, jax.numpy as jnp
        import numpy as np
        HEADS = 16
        MASKED_BIAS = -10000.0

        def _mha(q, k, v):
            B, Sq, D = q.shape
            Sk = k.shape[-2]
            hd = D // HEADS
            qh = q.reshape(B, Sq, HEADS, hd).transpose(0, 2, 1, 3)
            kh = k.reshape(B, Sk, HEADS, hd).transpose(0, 2, 1, 3)
            vh = v.reshape(B, Sk, HEADS, hd).transpose(0, 2, 1, 3)
            scores = jnp.einsum('bhqd,bhkd->bhqk', qh, kh) / math.sqrt(hd)
            qi = jnp.arange(Sq)[:, None] + (Sk - Sq)
            ki = jnp.arange(Sk)[None, :]
            causal = ki <= qi
            scores = jnp.where(causal[None, None], scores, jnp.asarray(MASKED_BIAS, scores.dtype))
            attn = jax.nn.softmax(scores, axis=-1)
            out = jnp.einsum('bhqk,bhkd->bhqd', attn, vh)
            return out.transpose(0, 2, 1, 3).reshape(B, Sq, D)
        key = jax.random.key(seed)
        kq, kk, kv = jax.random.split(key, 3)
        B, S, D = (4, 256, 512)
        q = jax.random.normal(kq, (B, S, D), dtype=jnp.float32)
        k = jax.random.normal(kk, (B, S, D), dtype=jnp.float32)
        v = jax.random.normal(kv, (B, S, D), dtype=jnp.float32)
        return {'q': q, 'k': k, 'v': v}
    _L0_xattn_all = _L0_xattn_setup()
    _L0_xattn_in = {k: v for k, v in _L0_xattn_all.items() if k in ()}
    del _L0_xattn_all

    def _L0_ffn_setup():
        import jax, jax.numpy as jnp
        import numpy as np
        DIM = 512
        N_EXPERTS = 8
        TOP_K = 2
        key = jax.random.key(seed)
        ks = jax.random.split(key, 5)
        x = jax.random.normal(ks[0], (4, 1024, DIM), dtype=jnp.float32)
        W_up = jax.random.normal(ks[1], (DIM, DIM), dtype=jnp.float32) * (1.0 / np.sqrt(DIM))
        W_down = jax.random.normal(ks[2], (DIM, DIM), dtype=jnp.float32) * (1.0 / np.sqrt(DIM))
        W_gate = jax.random.normal(ks[3], (N_EXPERTS, DIM), dtype=jnp.float32) * (1.0 / np.sqrt(DIM))
        W_expert = jax.random.normal(ks[4], (DIM, DIM), dtype=jnp.float32) * (1.0 / np.sqrt(DIM))
        return {'x': x, 'W_up': W_up, 'W_down': W_down, 'W_gate': W_gate, 'W_expert': W_expert}
    _L0_ffn_all = _L0_ffn_setup()
    _L0_ffn_in = {k: v for k, v in _L0_ffn_all.items() if k in ('W_up', 'W_down', 'W_gate', 'W_expert')}
    del _L0_ffn_all
    return {'x': x, 'ctx_2048': ctx_2048, 'L0_attn_q_w': _L0_attn_in['q_w'], 'L0_attn_q_b': _L0_attn_in['q_b'], 'L0_attn_k_w': _L0_attn_in['k_w'], 'L0_attn_k_b': _L0_attn_in['k_b'], 'L0_attn_v_w': _L0_attn_in['v_w'], 'L0_attn_v_b': _L0_attn_in['v_b'], 'L0_attn_o_w': _L0_attn_in['o_w'], 'L0_attn_o_b': _L0_attn_in['o_b'], 'L0_ffn_W_up': _L0_ffn_in['W_up'], 'L0_ffn_W_down': _L0_ffn_in['W_down'], 'L0_ffn_W_gate': _L0_ffn_in['W_gate'], 'L0_ffn_W_expert': _L0_ffn_in['W_expert']}

def reference(x, ctx_2048, L0_attn_q_w, L0_attn_q_b, L0_attn_k_w, L0_attn_k_b, L0_attn_v_w, L0_attn_v_b, L0_attn_o_w, L0_attn_o_b, L0_ffn_W_up, L0_ffn_W_down, L0_ffn_W_gate, L0_ffn_W_expert):
    import jax
    import jax.numpy as jnp

    def _L0_attn_ref(x, q_w, q_b, k_w, k_b, v_w, v_b, o_w, o_b):
        import jax, jax.numpy as jnp
        import numpy as np
        B, T, H, NH = (4, 512, 512, 16)
        HD = H // NH
        SCALE = HD ** (-0.5)
        Bd, Td, Hd = x.shape
        q = (x @ q_w.T + q_b).reshape(Bd, Td, NH, HD).transpose(0, 2, 1, 3)
        k = (x @ k_w.T + k_b).reshape(Bd, Td, NH, HD).transpose(0, 2, 1, 3)
        v = (x @ v_w.T + v_b).reshape(Bd, Td, NH, HD).transpose(0, 2, 1, 3)
        scores = jnp.einsum('bhqd,bhkd->bhqk', q, k) * SCALE
        causal = jnp.tril(jnp.ones((Td, Td), dtype=bool))
        scores = jnp.where(causal, scores, -jnp.inf)
        probs = jax.nn.softmax(scores, axis=-1)
        ctx = jnp.einsum('bhqk,bhkd->bhqd', probs, v)
        ctx = ctx.transpose(0, 2, 1, 3).reshape(Bd, Td, Hd)
        return ctx @ o_w.T + o_b

    def _L0_xattn_ref(q, k, v):
        import math
        import jax, jax.numpy as jnp
        import numpy as np
        HEADS = 16
        MASKED_BIAS = -10000.0

        def _mha(q, k, v):
            B, Sq, D = q.shape
            Sk = k.shape[-2]
            hd = D // HEADS
            qh = q.reshape(B, Sq, HEADS, hd).transpose(0, 2, 1, 3)
            kh = k.reshape(B, Sk, HEADS, hd).transpose(0, 2, 1, 3)
            vh = v.reshape(B, Sk, HEADS, hd).transpose(0, 2, 1, 3)
            scores = jnp.einsum('bhqd,bhkd->bhqk', qh, kh) / math.sqrt(hd)
            qi = jnp.arange(Sq)[:, None] + (Sk - Sq)
            ki = jnp.arange(Sk)[None, :]
            causal = ki <= qi
            scores = jnp.where(causal[None, None], scores, jnp.asarray(MASKED_BIAS, scores.dtype))
            attn = jax.nn.softmax(scores, axis=-1)
            out = jnp.einsum('bhqk,bhkd->bhqd', attn, vh)
            return out.transpose(0, 2, 1, 3).reshape(B, Sq, D)
        return _mha(q, k, v)

    def _L0_ffn_ref(x, W_up, W_down, W_gate, W_expert):
        import jax, jax.numpy as jnp
        import numpy as np
        DIM = 512
        N_EXPERTS = 8
        TOP_K = 2
        logits = jnp.einsum('bsd,ed->bse', x, W_gate)
        routing_weights, selected_experts = jax.lax.top_k(logits, TOP_K)
        shared_out = jnp.einsum('bsd,od->bso', jax.nn.relu(jnp.einsum('bsd,od->bso', x, W_up)), W_down)
        rw = jax.nn.softmax(routing_weights, axis=-1)
        expert_out = jnp.einsum('bsd,do->bso', x, W_expert)
        moe_out = jnp.sum(rw, axis=-1, keepdims=True) * expert_out
        return shared_out + moe_out
    x = x + _L0_attn_ref(_layernorm(x, axis=-1), L0_attn_q_w, L0_attn_q_b, L0_attn_k_w, L0_attn_k_b, L0_attn_v_w, L0_attn_v_b, L0_attn_o_w, L0_attn_o_b)
    x = x + _L0_xattn_ref(_layernorm(x, axis=-1), ctx_2048, ctx_2048)
    x = x + _L0_ffn_ref(_layernorm(x, axis=-1), L0_ffn_W_up, L0_ffn_W_down, L0_ffn_W_gate, L0_ffn_W_expert)
    return x

_drawn_inputs = setup_inputs


def setup_inputs(seed=0):
    import zlib

    import numpy as np

    out = dict(_drawn_inputs(seed))
    spreads = {'L0_attn_q_b': (0.0, 0.537),
     'L0_attn_k_b': (0.0, 0.8),
     'L0_attn_v_b': (0.0, 0.1),
     'L0_attn_o_b': (0.0, 0.1)}
    factors = {'L0_ffn_W_gate': 8.0}
    for name, (base, spread) in spreads.items():
        noise = np.random.default_rng([zlib.crc32(name.encode()), seed]).standard_normal(out[name].shape)
        drawn = base * np.exp(spread * noise) if base else spread * noise
        out[name] = jnp.asarray(drawn.astype(out[name].dtype))
    for name, factor in factors.items():
        out[name] = (out[name] * factor).astype(out[name].dtype)
    return out
```

```python
from contextlib import ExitStack

import concourse.bass as bass
from concourse import mybir

ALU = mybir.AluOpType
ACT = mybir.ActivationFunctionType
F32 = mybir.dt.float32
F32R = mybir.dt.float32r
BF16 = mybir.dt.bfloat16

B, T, D, NH = 4, 512, 512, 16
HD = D // NH
PART = 128
NT = T // PART
KC = D // PART
PAIRS = NH // 2
NE = 8
SCALE = HD ** -0.5
EPS = 1e-5
MASKED = -1.0e38
BIG = 3.0e38
RS = 3 * HD
QL, QH, KH, KL = range(4)


def f32(ap):
    return ap.bitcast(F32)


def wait_alone(eng, sem, value, passed):
    eng.wait_ge(sem, value)
    eng.sem_inc(passed, 1)


class Shared:
    pass


def split_weight(nc, sh, block_name, names, slots):
    with ExitStack() as ctx:
        raw = ctx.enter_context(nc.sbuf_tensor(f"raw_{block_name}", [PART, len(names), KC, D], F32))
        loaded = [ctx.enter_context(nc.semaphore(f"loaded_{n}")) for n in names]
        hi_done = ctx.enter_context(nc.semaphore(f"hi_{block_name}"))
        lo_done = ctx.enter_context(nc.semaphore(f"lo_{block_name}"))
        block = ctx.enter_context(nc.Block())

        @block.sync
        def _(sp):
            for i, name in enumerate(names):
                sp.dma_start(raw[:, i], sh.dram[name].rearrange("(c p) n -> p c n", p=PART)).then_inc(loaded[i], 16)

        @block.scalar
        def _(act):
            for i, s in enumerate(slots):
                act.wait_ge(loaded[i], 16)
                nc.scalar.activation(sh.w_hi[:, s], raw[:, i], ACT.Copy).then_inc(hi_done, 1)

        @block.vector
        def _(dve):
            for i, s in enumerate(slots):
                dve.wait_ge(hi_done, i + 1)
                nc.vector.tensor_tensor(sh.w_lo[:, s], raw[:, i], f32(sh.w_hi[:, s]), ALU.subtract)\
                    .then_inc(lo_done, 1)
            dve.wait_ge(lo_done, len(slots))


def attention(nc, sh, cross):
    tag = "x" if cross else "s"
    x_in, x_out = (sh.dram["x2"], sh.dram["x3"]) if cross else (sh.dram["x"], sh.dram["x2"])
    x_in = x_in.rearrange("(b t p) n -> b p t n", b=B, p=PART)
    x_out = x_out.rearrange("(b t p) n -> b p t n", b=B, p=PART)
    w_hi, w_lo = sh.w_hi, sh.w_lo
    WQ, WK, WV, WO = range(4)

    with ExitStack() as ctx:
        def sb(name, shape, dt=F32):
            return ctx.enter_context(nc.sbuf_tensor(f"{tag}_{name}", shape, dt))

        def sem(name):
            return ctx.enter_context(nc.semaphore(f"{tag}_{name}"))

        xt = sb("xt", [PART, NT, D])
        xln = sb("xln", [PART, NT, D]) if cross else xt
        xres = sb("xres", [PART, NT, D])
        stage = sb("stage", [PART, 2, 4, T], F32R)
        stack = sb("stack", [PART, 4, 2, 2, T], F32R)
        V = sb("V", [PART, NT, D])
        prob = [sb(f"prob{kb}", [PART, 4, T - PART * kb]) for kb in range(NT)]
        junk = sb("junk", [PART, 2, T], BF16)
        negmax = sb("negmax", [PART, 2, 2, NT])
        st = sb("st", [PART, 2, 2, NT, RS + 2], F32R)
        rden = sb("rden", [PART, T])
        cn = sb("cn", [PART, T])
        stats = sb("stats", [PART, NT, 6])
        mv = sb("mv", [PART, NT, 2])
        veps = sb("veps", [PART, NT])
        rstd = sb("rstd", [PART, NT])
        if cross:
            kraw = sb("kraw", [PART, 2, T])
        else:
            xT_hi = sb("xT_hi", [PART, KC, T], F32R)
            xT_lo = sb("xT_lo", [PART, KC, T], F32R)
            cx_hi = sb("cx_hi", [PART, KC, T], F32R)
            cx_lo = sb("cx_lo", [PART, KC, T], F32R)

        def bank(name):
            return ctx.enter_context(nc.psum_tensor(f"{tag}_{name}", [PART, T], F32))

        s_bank = [bank("s0"), bank("s1")]
        t_bank = [bank("t0"), bank("t1")]
        pv_bank, den_bank, m6, m7 = bank("pv"), bank("den"), bank("m6"), bank("m7")

        x_loaded = sem("x_loaded")
        res_loaded = sem("res_loaded")
        res_biased = sem("res_biased")
        stored = sem("stored")
        v_loaded = sem("v_loaded")
        kraw_in = [sem("kraw_in0"), sem("kraw_in1")]
        stack_in = [sem(f"stack_in{i}") for i in range(4)]
        dve_passed, pool_passed, sp_passed = sem("dve_passed"), sem("pool_passed"), sem("sp_passed")
        init = sem("init")
        ln_stat = sem("ln_stat")
        ln_mv = sem("ln_mv")
        ln_eps = sem("ln_eps")
        ln_rstd = sem("ln_rstd")
        ln_done = sem("ln_done")
        lnt_mm = sem("lnt_mm")
        lnt_hi = sem("lnt_hi")
        lnt_lo = sem("lnt_lo")
        q_mm, k_mm = sem("q_mm"), sem("k_mm")
        q_hi, k_hi = sem("q_hi"), sem("k_hi")
        q_lo, k_lo = sem("q_lo"), sem("k_lo")
        s_mm = sem("s_mm")
        s_max = sem("s_max")
        st_hi, st_lo = sem("st_hi"), sem("st_lo")
        z_mm = sem("z_mm")
        z_in = sem("z_in")
        t_mm = sem("t_mm")
        e_done = sem("e_done")
        tri_done = sem("tri_done")
        pv_done = sem("pv_done")
        rd_done = sem("rd_done")
        norm_done = sem("norm_done")
        cx_hi_done, cx_lo_done = sem("cx_hi_done"), sem("cx_lo_done")
        row_mm = sem("row_mm")
        row_done = sem("row_done")

        E0, PV0, N0, T0, CX0, R0 = 2, NT, 1, 1, 1, int(cross)

        block = ctx.enter_context(nc.Block())

        def sp_stack(sp, b, p):
            q = p + 3
            g = q // 2
            slot = q % 4
            sp.wait_ge(q_lo, KC * b + g + 1)
            sp.wait_ge(k_lo, KC * b + g + 1)
            if p >= 0:
                sp.wait_ge(t_mm, T0 + PAIRS * (PAIRS * b + p))
            for h in range(2):
                j = 2 * (q % 2) + h
                src = stage[HD * j:HD * j + HD, g % 2]
                for r, pick in enumerate((slice(QH, KH + 1), slice(QH, KL + 1, 2), slice(QL, KH + 1, 2))):
                    sp.dma_start(f32(stack[HD * r:HD * r + HD, slot, h, :, :]), f32(src[:, pick, :]))\
                        .then_inc(stack_in[slot], 16)

        def stack_ready(b, p):
            return 96 * (2 * b + p // 4 + 1)

        def sp_kraw(sp, b, g):
            if not (isinstance(b, int) and KC * b + g < 2):
                sp.wait_ge(k_lo, KC * b + g - 1)
            bb, gg = b + g // KC, g % KC
            sp.dma_start(kraw[:, g % 2, :], sh.dram["ctxT"].rearrange("(b c p) n -> b p c n", b=B, p=PART)[bb, :, gg, :])\
                .then_inc(kraw_in[g % 2], 16)

        def sp_v(sp, b):
            sp.dma_start(V[:, :, :], sh.dram["ctx"].rearrange("(b t p) n -> b p t n", b=B, p=PART)[b])\
                .then_inc(v_loaded, 16)

        @block.sync
        def _(sp):
            sp.dma_start(xt[:, :, :], x_in[0]).then_inc(x_loaded, 16)
            if cross:
                sp_kraw(sp, 0, 0)
                sp_kraw(sp, 0, 1)
                sp_v(sp, 0)
            sp.dma_start(xres[:, :, :], x_in[0]).then_inc(res_loaded, 16)
            for p in range(-3, 0):
                sp_stack(sp, 0, p)
                if cross and p == -3:
                    sp_kraw(sp, 0, 2)

            def batch(b, last):
                for p in range(PAIRS):
                    if p < 5 or not last:
                        sp_stack(sp, b, p)
                    if cross and p % 2 == 0 and not (last and p >= 2):
                        sp_kraw(sp, b, p // 2 + 3)
                    if p == 0 and not last:
                        sp.wait_ge(ln_done if cross else lnt_mm, KC * (b + 1))
                        sp.dma_start(xt[:, :, :], x_in[b + 1]).then_inc(x_loaded, 16)
                if cross and not last:
                    sp.wait_ge(pv_done, PV0 + NT * KC * (b + 1))
                    sp_v(sp, b + 1)
                wait_alone(sp, row_done, R0 + KC * (b + 1) if cross else 2 * NT * (b + 1) + (0 if last else NT),
                           sp_passed)
                sp.dma_start(x_out[b], xres[:, :, :]).then_inc(stored, 16)
                sp.wait_ge(stored, 16 * (b + 1))
                if not last:
                    sp.dma_start(xres[:, :, :], x_in[b + 1]).then_inc(res_loaded, 16)

            with sp.Fori(0, B - 1) as b:
                batch(b, False)
            batch(B - 1, True)

        def mm3(out, lhs, rhs, first, last):
            (lh, ll), (rh, rl) = lhs, rhs
            nc.tensor.matmul(out, ll, rh, start=first, stop=False)
            nc.tensor.matmul(out, lh, rl, start=False, stop=False)
            return nc.tensor.matmul(out, lh, rh, start=False, stop=last)

        def pe_s(pe, b, p, i):
            h, qb = divmod(i, NT)
            slot = p % 4
            n = PAIRS * (PAIRS * b + p) + i
            if i == 0:
                pe.wait_ge(stack_in[slot], stack_ready(b, p))
            if not (isinstance(n, int) and n < 2):
                pe.wait_ge(s_max, n - 1)
            N = PART * (qb + 1)
            nc.tensor.matmul(s_bank[i % 2][:, 0:N], stack[0:RS, slot, h, 0, PART * qb:PART * qb + PART],
                             stack[0:RS, slot, h, 1, 0:N], start=True, stop=True).then_inc(s_mm, 1)

        def pe_z(pe, b, p, h, before):
            pe.wait_ge(st_lo, 2 * (PAIRS * b + p) + h + 1)
            before(pe)
            for qb in range(NT):
                mm = nc.tensor.matmul(m7[0:RS + 2, PART * qb:PART * qb + PART], st[:, p % 2, h, qb, :],
                                      sh.ident_r[:, :], start=True, stop=True)
            mm.then_inc(z_mm, 1)

        def pe_t(pe, b, p, i):
            kb, h = divmod(i, 2)
            slot = p % 4
            n = PAIRS * (PAIRS * b + p) + i
            if i < 2:
                pe.wait_ge(z_in, 2 * (PAIRS * b + p) + h + 1)
            pe.wait_ge(e_done, E0 + n - 1)
            nc.tensor.matmul(t_bank[i % 2][:, 0:T - PART * kb], stack[0:RS + 2, slot, h, 1, PART * kb:PART * kb + PART],
                             stack[0:RS + 2, slot, h, 0, PART * kb:T], start=True, stop=True).then_inc(t_mm, 1)

        def pe_pv(pe, b, g, kb):
            G = KC * b + g
            if kb == 0:
                pe.wait_ge(norm_done, N0 + G)
                if cross:
                    pe.wait_ge(v_loaded, 16 * (b + 1))
                elif g == 0:
                    pe.wait_ge(row_done, 2 * NT * b + NT)
            pe.wait_ge(tri_done, NT * (2 * G + 1) + kb + 1)
            for j in range(4):
                nc.tensor.matmul(pv_bank[HD * j:HD * j + HD, PART * kb:T],
                                 V[:, kb, PART * g + HD * j:PART * g + HD * j + HD], prob[kb][:, j, :],
                                 start=(kb == 0), stop=(kb == NT - 1))
            for j in range(4):
                mm = nc.tensor.matmul(den_bank[HD * j:HD * j + HD, PART * kb:T], sh.ones[:, 0:HD], prob[kb][:, j, :],
                                      start=(kb == 0), stop=(kb == NT - 1))
            mm.then_inc(pv_done, 1)

        def pe_qk(pe, b, p, part, before):
            g = (p + 5) // 2
            half = (p + 1) % 2
            if cross:
                if half == 0 and part == 0:
                    before(pe)
                    if g % KC == 0:
                        pe.wait_ge(ln_done, NT * (b + g // KC + 1))
                    for t in range(NT):
                        mm = nc.tensor.transpose(m6[:, PART * t:PART * t + PART],
                                                 xln[:, t, PART * (g % KC):PART * (g % KC) + PART], sh.ident[:, :])
                    mm.then_inc(q_mm, 1)
                return
            if part == 0:
                before(pe)
                if g % KC == 0 and half == 0:
                    pe.wait_ge(lnt_lo, KC * (b + g // KC + 1))
            w = WK if half else WQ
            for n in (2 * part, 2 * part + 1):
                c, term = divmod(n, 3)
                cols = slice(PART * (g % KC), PART * (g % KC) + PART)
                wh, wl, xh, xl = w_hi[:, w, c, cols], w_lo[:, w, c, cols], xT_hi[:, c, :], xT_lo[:, c, :]
                lhs, rhs = ((wl, xh), (wh, xl), (wh, xh))[term]
                mm = nc.tensor.matmul(m6[:, :], lhs, rhs, start=(n == 0), stop=(n == 11))
            if part == 5:
                mm.then_inc(k_mm if half else q_mm, 1)

        def pe_lnt(pe, b, c, before):
            out = (m6, m7)[c % 2]
            before(pe)
            for t in range(NT):
                mm = nc.tensor.transpose(out[:, PART * t:PART * t + PART], xln[:, t, PART * c:PART * c + PART],
                                         sh.ident[:, :])
            mm.then_inc(lnt_mm, 1)

        def pe_rows(pe, lhs, w, t, before):
            before(pe)
            out = (m6, m7)[t % 2]
            for c in range(KC):
                mm = mm3(out[:, :], (lhs[0][:, c, PART * t:PART * t + PART], lhs[1][:, c, PART * t:PART * t + PART]),
                         (w_hi[:, w, c, :], w_lo[:, w, c, :]), c == 0, c == KC - 1)
            mm.then_inc(row_mm, 1)

        def pe_back(pe, b, g, last):
            G = KC * b + g
            pe.wait_ge(norm_done, N0 + G + 1)
            pe.wait_ge(z_in, 2 * (PAIRS * b + min(2 * g + 5, PAIRS + (0 if last else 1))))
            pe.wait_ge(row_done, R0 + G)
            for t in range(NT):
                mm = nc.tensor.transpose(m7[:, PART * t:PART * t + PART], cn[:, PART * t:PART * t + PART],
                                         sh.ident[:, :])
            mm.then_inc(row_mm, 1)

        @block.tensor
        def _(pe):
            pe.wait_ge(init, 2)
            pe.sem_inc(t_mm, T0)
            pe.sem_inc(pv_done, PV0)

            def m6_free(b, p):
                if cross:
                    def w(pe):
                        G = KC * b + (p + 5) // 2
                        if isinstance(G, int) and G == 0:
                            return
                        pe.wait_ge(q_lo, G)
                    return w

                def w(pe):
                    g, half = (p + 5) // 2, (p + 1) % 2
                    if p == 0:
                        pe.wait_ge(row_done, NT + 2 * NT * b)
                        return
                    if (isinstance(b, int) and p == -5) or (p == 3):
                        pe.wait_ge(lnt_lo, KC * (b + 1) if p < 0 else KC * (b + 2))
                        return
                    if half:
                        pe.wait_ge(q_lo, KC * b + g + 1)
                    else:
                        pe.wait_ge(k_lo, KC * b + g)
                return w

            def step(b, p, s_, z_, t_, qk_):
                for i in range(PAIRS):
                    if s_:
                        pe_s(pe, b, p + 2, i)
                    if t_:
                        pe_t(pe, b, p, i)
                    if z_ and i in (2, 5):
                        h = 0 if i == 2 else 1
                        n = 2 * (PAIRS * b + p + 1) + h

                        def m7_free(pe):
                            if h == 0 and cross and p == 0:
                                pe.wait_ge(row_done, R0 + KC * b)
                            elif h == 0 and cross and p in (4, 6):
                                pe.wait_ge(row_done, R0 + KC * b + p // 2 - 1)
                            elif h == 0 and not cross and p == 0:
                                pe.wait_ge(row_done, NT + 2 * NT * b)
                            elif h == 0 and not cross and p == -1:
                                pe.wait_ge(lnt_lo, KC)
                            elif h == 0 and not cross and p == 3 and qk_:
                                pe.wait_ge(lnt_lo, KC * (b + 2))
                            elif not (isinstance(n, int) and n == 0):
                                pe.wait_ge(z_in, n)
                        pe_z(pe, b, p + 1, h, m7_free)
                    if t_ and p % 2 == 1 and i in (4, 7):
                        pe_pv(pe, b, p // 2, i // 7)
                    if t_ and p % 2 == 0 and p > 0 and i in (1, 3):
                        pe_pv(pe, b, p // 2 - 1, 2 + i // 2)
                    if cross and t_ and p % 2 == 1 and p > 1 and i == 7:
                        pe_back(pe, b, p // 2 - 1, not z_)
                    if qk_ and 1 <= i <= 6:
                        pe_qk(pe, b, p, i - 1, m6_free(b, p))

            def lnt(b, prologue):
                for c in range(KC):
                    def w(pe):
                        if c == 0:
                            pe.wait_ge(ln_done, NT * (b + 1))
                            if not prologue:
                                pe.wait_ge(k_lo, KC * b)
                        elif c == 1 and not prologue:
                            pe.wait_ge(z_in, 2 * (PAIRS * (b - 1) + 4))
                        elif c >= 2:
                            pe.wait_ge(lnt_lo, KC * b + c - 1)
                    pe_lnt(pe, b, c, w)

            def v_tiles(b, base):
                for t in range(NT):
                    def w(pe):
                        if t == 0:
                            pe.wait_ge(q_lo, KC * b + 3)
                        elif t == 1:
                            pe.wait_ge(z_in, 2 * (PAIRS * b + 1))
                        else:
                            pe.wait_ge(row_done, base + t - 1)
                    pe_rows(pe, (xT_hi, xT_lo), WV, t, w)

            if not cross:
                lnt(0, True)
            for p in range(-5, 0):
                step(0, p, p >= -2, p >= -1, False, True)
            if not cross:
                v_tiles(0, 0)

            def batch(b, last):
                for p in range(PAIRS):
                    if p == 3 and not cross and not last:
                        lnt(b + 1, False)
                    step(b, p, p < 6 or not last, p < 7 or not last, True, p < 3 or not last)
                pe_pv(pe, b, KC - 1, 2)
                pe_pv(pe, b, KC - 1, 3)
                if cross:
                    pe_back(pe, b, KC - 1, last)
                    return
                if not last:
                    v_tiles(b + 1, NT + 2 * NT * b)
                base = NT + 2 * NT * b + (0 if last else NT)
                for t in range(NT):
                    def w(pe):
                        if t == 0:
                            pe.wait_ge(cx_hi_done, KC * (b + 1))
                            pe.wait_ge(cx_lo_done, CX0 + KC * (b + 1))
                        if last and t == 0:
                            pe.wait_ge(k_lo, KC * (b + 1))
                        elif last and t == 1:
                            pe.wait_ge(z_in, 2 * PAIRS * (b + 1))
                        else:
                            pe.wait_ge(row_done, base + t - 1)
                    pe_rows(pe, (cx_hi, cx_lo), WO, t, w)

            with pe.Fori(0, B - 1) as b:
                batch(b, False)
            batch(B - 1, True)

        def dve_s(dve, b, p, i):
            h, qb = divmod(i, NT)
            n = PAIRS * (PAIRS * b + p) + i
            N = PART * (qb + 1)
            wait_alone(dve, s_mm, n + 1, dve_passed)
            nc.vector.tensor_tensor_reduce(junk[:, i % 2, 0:N], s_bank[i % 2][:, 0:N], sh.mask[:, T - N:T], -1.0, BIG,
                                           ALU.add, ALU.min, negmax[:, p % 2, h, qb:qb + 1]).then_inc(s_max, 1)
            if qb == NT - 1:
                m = 2 * (PAIRS * b + p) + h
                dve.wait_ge(s_max, n + 1)
                if not (isinstance(m, int) and m < 4):
                    dve.wait_ge(z_mm, m - 3)
                nc.vector.tensor_copy(st[:, p % 2, h, :, RS], negmax[:, p % 2, h, :]).then_inc(st_hi, 1)
                dve.wait_ge(st_hi, m + 1)
                nc.vector.tensor_tensor(st[:, p % 2, h, :, RS + 1], negmax[:, p % 2, h, :],
                                        f32(st[:, p % 2, h, :, RS]), ALU.subtract).then_inc(st_lo, 1)

        def dve_qk(dve, b, p):
            g, half = (p + 5) // 2, (p + 1) % 2
            G = KC * b + g
            if cross and half:
                return
            dve.wait_ge(k_hi if half else q_hi, G + 1)
            out = stage[:, g % 2, KL if half else QL, :]
            hi = f32(stage[:, g % 2, KH if half else QH, :])
            if cross:
                nc.vector.tensor_tensor(out, m6[:, :], hi, ALU.subtract).then_inc(q_lo, 1)
            else:
                nc.vector.scalar_tensor_tensor(out=out, in0=m6[:, :], scalar=sh.qkb[:, half, g % KC:g % KC + 1],
                                               in1=hi, op0=ALU.add, op1=ALU.subtract)\
                    .then_inc(k_lo if half else q_lo, 1)

        def dve_ln_stats(dve, b, t):
            if t == 0:
                dve.wait_ge(x_loaded, 16 * (b + 1))
            nc.vector.bn_stats(stats[:, t, :], xt[:, t, :]).then_inc(ln_stat, 1)
            wait_alone(dve, ln_stat, NT * b + t + 1, dve_passed)
            nc.vector.bn_aggr(mv[:, t, :], stats[:, t, :]).then_inc(ln_mv, 1)

        def dve_ln_norm(dve, b, t):
            if t == 0:
                dve.wait_ge(ln_rstd, b + 1)
            nc.vector.tensor_scalar(xln[:, t, :], xt[:, t, :], mv[:, t, 0:1], rstd[:, t:t + 1],
                                    ALU.subtract, ALU.mult).then_inc(ln_done, 1)

        def dve_lnt(dve, b, c):
            dve.wait_ge(lnt_hi, KC * b + c + 1)
            nc.vector.tensor_tensor(xT_lo[:, c, :], (m6, m7)[c % 2][:, :], f32(xT_hi[:, c, :]), ALU.subtract)\
                .then_inc(lnt_lo, 1)

        def dve_recip(dve, b, g, quarter):
            G = KC * b + g
            if quarter == 0:
                dve.wait_ge(pv_done, PV0 + NT * (G + 1))
            cols = slice(PART * quarter, PART * quarter + PART)
            nc.vector.reciprocal(rden[:, cols], den_bank[:, cols]).then_inc(rd_done, 1)

        def dve_norm(dve, b, g):
            G = KC * b + g
            dve.wait_ge(rd_done, NT * (G + 1))
            if cross:
                dve.wait_ge(row_mm, R0 + G)
            else:
                dve.wait_ge(cx_lo_done, CX0 + G)
            nc.vector.tensor_tensor(cn[:, :], pv_bank[:, :], rden[:, :], ALU.mult).then_inc(norm_done, 1)

        def dve_back(dve, b, g):
            G = KC * b + g
            dve.wait_ge(row_mm, R0 + G + 1)
            if g == 0:
                dve.wait_ge(res_loaded, 16 * (b + 1))
            cols = slice(PART * g, PART * g + PART)
            nc.vector.tensor_tensor(xres[:, :, cols], m7[:, :].rearrange("p (t n) -> p t n", t=NT), xres[:, :, cols],
                                    ALU.add).then_inc(row_done, 1)

        @block.vector
        def _(dve):
            nc.vector.memset(f32(st[:, :, :, :, :]), 0.0).then_inc(init, 1)
            nc.vector.memset(f32(stack[RS:RS + 2, :, :, 1, :]), 1.0).then_inc(init, 1)
            dve.sem_inc(norm_done, N0)
            if cross:
                dve.sem_inc(row_done, R0)
                dve.sem_inc(row_mm, R0)
            dve.wait_ge(init, 2)

            def step(b, p, s_, qk_, att_):
                for i in range(PAIRS):
                    if s_:
                        dve_s(dve, b, p + 2, i)
                    if att_ and p % 2 == 0 and p > 0 and i >= 4:
                        dve_recip(dve, b, p // 2 - 1, i - 4)
                    if qk_ and p == 1 and i >= 4:
                        dve_ln_stats(dve, b + 1, i - 4)
                    if qk_ and p == 2 and i >= 4:
                        if i == 4 and cross:
                            dve.wait_ge(q_mm, KC * (b + 1))
                        dve_ln_norm(dve, b + 1, i - 4)
                if cross and att_ and p % 2 == 1 and p > 1:
                    dve_back(dve, b, p // 2 - 1)
                if att_ and p % 2 == 0 and p > 0:
                    dve_norm(dve, b, p // 2 - 1)
                if qk_ or (att_ and p < 3):
                    dve_qk(dve, b, p)

            for t in range(NT):
                dve_ln_stats(dve, 0, t)
            for t in range(NT):
                dve_ln_norm(dve, 0, t)
            if not cross:
                for c in range(KC):
                    dve_lnt(dve, 0, c)
            for p in range(-5, 0):
                step(0, p, p >= -2, True, False)

            def rows(t, add, out, base):
                dve.wait_ge(row_mm, base + t + 1)
                nc.vector.tensor_tensor(out, (m6, m7)[t % 2][:, :], add, ALU.add).then_inc(row_done, 1)

            if not cross:
                for t in range(NT):
                    rows(t, sh.v_bias[:, :], V[:, t, :], 0)

            def batch(b, last):
                for p in range(PAIRS):
                    if p == 3 and not cross and not last:
                        for c in range(KC):
                            dve_lnt(dve, b + 1, c)
                    step(b, p, p < 6 or not last, not last, True)
                for q in range(NT):
                    dve_recip(dve, b, KC - 1, q)
                dve_norm(dve, b, KC - 1)
                if cross:
                    dve_back(dve, b, KC - 1)
                    return
                base = NT + 2 * NT * b
                if not last:
                    for t in range(NT):
                        rows(t, sh.v_bias[:, :], V[:, t, :], base)
                    base = base + NT
                dve.wait_ge(res_biased, NT * (b + 1))
                for t in range(NT):
                    rows(t, xres[:, t, :], xres[:, t, :], base)

            with dve.Fori(0, B - 1) as b:
                batch(b, False)
            batch(B - 1, True)

        def act_exp(act, b, p, i):
            kb, h = divmod(i, 2)
            P = PAIRS * b + p
            act.wait_ge(t_mm, T0 + PAIRS * P + i + 1)
            act.wait_ge(pv_done, PV0 + NT * (KC * b + p // 2 - 1) + kb + 1)
            nc.scalar.activation(prob[kb][:, 2 * (p % 2) + h, :], t_bank[i % 2][:, 0:T - PART * kb], ACT.Exp,
                                 scale=SCALE).then_inc(e_done, 1)

        def act_z(act, b, p, h):
            act.wait_ge(z_mm, 2 * (PAIRS * b + p) + h + 1)
            nc.scalar.activation(stack[RS:RS + 2, p % 4, h, 0, :], m7[RS:RS + 2, :], ACT.Copy).then_inc(z_in, 1)

        def act_qk(act, b, p):
            g, half = (p + 5) // 2, (p + 1) % 2
            G = KC * b + g
            out = stage[:, g % 2, KH if half else QH, :]
            q = 2 * g - 3
            if not (isinstance(b, int) and PAIRS * b + q < 0):
                act.wait_ge(stack_in[q % 4], stack_ready(b, q))
            if cross:
                if half:
                    act.wait_ge(kraw_in[g % 2], 16 * (2 * b + g // 2 + 1))
                    nc.scalar.activation(out, kraw[:, g % 2, :], ACT.Copy).then_inc(k_hi, 1)
                else:
                    act.wait_ge(q_mm, G + 1)
                    nc.scalar.activation(out, m6[:, :], ACT.Copy).then_inc(q_hi, 1)
            else:
                act.wait_ge(k_mm if half else q_mm, G + 1)
                nc.scalar.activation(out, m6[:, :], ACT.Identity, bias=sh.qkb[:, half, g % KC:g % KC + 1])\
                    .then_inc(k_hi if half else q_hi, 1)

        def act_lnt(act, b, c):
            act.wait_ge(lnt_mm, KC * b + c + 1)
            nc.scalar.activation(xT_hi[:, c, :], (m6, m7)[c % 2][:, :], ACT.Copy).then_inc(lnt_hi, 1)

        def act_cx(act, b, g):
            G = KC * b + g
            act.wait_ge(norm_done, N0 + G + 1)
            if g == 0:
                act.wait_ge(row_mm, NT + 2 * NT * b)
            nc.scalar.activation(cx_hi[:, g, :], cn[:, :], ACT.Copy).then_inc(cx_hi_done, 1)

        @block.scalar
        def _(act):
            act.sem_inc(e_done, E0)

            def step(b, p, z_, t_, qk_):
                for i in range(PAIRS):
                    if t_:
                        act_exp(act, b, p, i)
                    if z_ and i in (2, 5):
                        act_z(act, b, p + 1, 0 if i == 2 else 1)
                if qk_:
                    act_qk(act, b, p)
                if not cross and t_ and p % 2 == 0 and p > 0:
                    act_cx(act, b, p // 2 - 1)

            if not cross:
                for c in range(KC):
                    act_lnt(act, 0, c)
            for p in range(-5, 0):
                step(0, p, p >= -1, False, True)

            def batch(b, last):
                for p in range(PAIRS):
                    if p == 3 and not cross and not last:
                        for c in range(KC):
                            act_lnt(act, b + 1, c)
                    step(b, p, p < 7 or not last, True, p < 3 or not last)
                if not cross:
                    act_cx(act, b, KC - 1)

            with act.Fori(0, B - 1) as b:
                batch(b, False)
            batch(B - 1, True)

        def pool_tri(pool, b, p, kb):
            P = PAIRS * b + p
            wait_alone(pool, e_done, E0 + PAIRS * P + 2 * kb + 2, pool_passed)
            j = 2 * (p % 2)
            d = prob[kb][:, j:j + 2, 0:PART]
            nc.gpsimd.affine_select(out=d, in_=d, pattern=[[0, 2], [1, PART]], compare_op=ALU.is_ge, fill=0.0,
                                    base=0, channel_multiplier=-1).then_inc(tri_done, 1)

        def pool_rstd(pool, b):
            wait_alone(pool, ln_mv, NT * (b + 1), pool_passed)
            nc.gpsimd.tensor_scalar(veps[:, :], mv[:, :, 1], EPS, None, ALU.add).then_inc(ln_eps, 1)
            pool.wait_ge(ln_eps, b + 1)
            nc.gpsimd.tensor_tensor(rstd[:, :], veps[:, :], sh.neg_half[:, 0:NT], ALU.pow).then_inc(ln_rstd, 1)

        def pool_k(pool, b, p):
            g = (p + 5) // 2
            G = KC * b + g
            pool.wait_ge(k_hi, G + 1)
            nc.gpsimd.tensor_tensor(stage[:, g % 2, KL, :], kraw[:, g % 2, :], f32(stage[:, g % 2, KH, :]),
                                    ALU.subtract).then_inc(k_lo, 1)

        def pool_cx(pool, b, g):
            pool.wait_ge(cx_hi_done, KC * b + g + 1)
            nc.gpsimd.tensor_tensor(cx_lo[:, g, :], cn[:, :], f32(cx_hi[:, g, :]), ALU.subtract)\
                .then_inc(cx_lo_done, 1)

        @block.gpsimd
        def _(pool):
            if not cross:
                pool.sem_inc(cx_lo_done, CX0)
            pool_rstd(pool, 0)

            def step(b, p, t_, qk_, ln_):
                if t_:
                    for kb in range(NT):
                        pool_tri(pool, b, p, kb)
                if cross and qk_ and (p + 1) % 2:
                    pool_k(pool, b, p)
                if ln_:
                    pool_rstd(pool, b + 1)
                if not cross and t_ and p % 2 == 0 and p > 0:
                    pool_cx(pool, b, p // 2 - 1)
                if not cross and t_ and 3 <= p < 7:
                    if p == 3:
                        pool.wait_ge(res_loaded, 16 * (b + 1))
                    nc.gpsimd.tensor_tensor(xres[:, p - 3, :], xres[:, p - 3, :], sh.o_bias[:, :], ALU.add)\
                        .then_inc(res_biased, 1)

            for p in range(-5, 0):
                step(0, p, False, True, False)

            def batch(b, last):
                for p in range(PAIRS):
                    step(b, p, True, p < 3 or not last, p == 1 and not last)
                if not cross:
                    pool_cx(pool, b, KC - 1)

            with pool.Fori(0, B - 1) as b:
                batch(b, False)
            batch(B - 1, True)


def ffn(nc, sh):
    x_in = sh.dram["x3"].rearrange("(b t p) n -> b p t n", b=B, p=PART)
    x_out = sh.dram["out"].rearrange("(b t p) n -> b p t n", b=B, p=PART)
    w_hi, w_lo = sh.w_hi, sh.w_lo
    UP, DOWN, EXPERT = range(3)
    with ExitStack() as ctx:
        def sb(name, shape, dt=F32):
            return ctx.enter_context(nc.sbuf_tensor(f"f_{name}", shape, dt))

        def sem(name):
            return ctx.enter_context(nc.semaphore(f"f_{name}"))

        xt = sb("xt", [PART, NT, D])
        xln = sb("xln", [PART, NT, D])
        xres = sb("xres", [PART, NT, D])
        xT_hi = sb("xT_hi", [PART, KC, T], F32R)
        xT_lo = sb("xT_lo", [PART, KC, T], F32R)
        h_hi = sb("h_hi", [PART, KC, T], F32R)
        h_lo = sb("h_lo", [PART, KC, T], F32R)
        stats = sb("stats", [PART, NT, 6])
        mv = sb("mv", [PART, NT, 2])
        veps = sb("veps", [PART, NT])
        rstd = sb("rstd", [PART, NT])
        logits = sb("logits", [PART, NT, NE])
        top = sb("top", [PART, NT, 8])
        gap = sb("gap", [PART, NT])
        e2 = sb("e2", [PART, NT])
        den = sb("den", [PART, NT])
        rw1 = sb("rw1", [PART, NT])
        rw2 = sb("rw2", [PART, NT])
        rw = sb("rw", [PART, NT])
        bank = [ctx.enter_context(nc.psum_tensor(f"f_b{i}", [PART, T], F32)) for i in range(8)]
        T_BANK, UP_BANK, GATE_BANK, DOWN_BANK, EXP_BANK = bank[0:2], bank[0:2], bank[2], bank[4:6], bank[6:8]

        x_loaded, res_loaded, stored = sem("x_loaded"), sem("res_loaded"), sem("stored")
        ln_stat, ln_mv, ln_eps, ln_rstd, ln_done = (sem(n) for n in ("ln_stat", "ln_mv", "ln_eps", "ln_rstd",
                                                                     "ln_done"))
        lnt_mm, lnt_hi, lnt_lo = sem("lnt_mm"), sem("lnt_hi"), sem("lnt_lo")
        up_mm, h_hi_done, h_lo_done = sem("up_mm"), sem("h_hi_done"), sem("h_lo_done")
        gate_mm, gate_out = sem("gate_mm"), sem("gate_out")
        g_step = sem("g_step")
        e2_done = sem("e2_done")
        down_mm, exp_mm, y_mid, y_done = sem("down_mm"), sem("exp_mm"), sem("y_mid"), sem("y_done")
        dve_passed, pool_passed = sem("dve_passed"), sem("pool_passed")
        GSTEPS = NT + 5

        block = ctx.enter_context(nc.Block())

        @block.sync
        def _(sp):
            sp.dma_start(xt[:, :, :], x_in[0]).then_inc(x_loaded, 16)
            sp.dma_start(xres[:, :, :], x_in[0]).then_inc(res_loaded, 16)

            def batch(b, last):
                if not last:
                    sp.wait_ge(ln_done, NT * (b + 1))
                    sp.dma_start(xt[:, :, :], x_in[b + 1]).then_inc(x_loaded, 16)
                sp.wait_ge(y_done, NT * (b + 1))
                sp.dma_start(x_out[b], xres[:, :, :]).then_inc(stored, 16)
                sp.wait_ge(stored, 16 * (b + 1))
                if not last:
                    sp.dma_start(xres[:, :, :], x_in[b + 1]).then_inc(res_loaded, 16)

            with sp.Fori(0, B - 1) as b:
                batch(b, False)
            batch(B - 1, True)

        @block.tensor
        def _(pe):
            def three(out, lhs, rhs, first, last):
                nc.tensor.matmul(out, lhs[1], rhs[0], start=first, stop=False)
                nc.tensor.matmul(out, lhs[0], rhs[1], start=False, stop=False)
                return nc.tensor.matmul(out, lhs[0], rhs[0], start=False, stop=last)

            with pe.Fori(0, B) as b:
                for c in range(KC):
                    if c == 0:
                        pe.wait_ge(ln_done, NT * (b + 1))
                    if c >= 2:
                        pe.wait_ge(lnt_lo, KC * b + c - 1)
                    for t in range(NT):
                        mm = nc.tensor.transpose(T_BANK[c % 2][:, PART * t:PART * t + PART],
                                                 xln[:, t, PART * c:PART * c + PART], sh.ident[:, :])
                    mm.then_inc(lnt_mm, 1)
                pe.wait_ge(lnt_lo, KC * (b + 1))
                for m in range(KC):
                    if m >= 2:
                        pe.wait_ge(h_lo_done, KC * b + m - 1)
                    for c in range(KC):
                        cols = slice(PART * m, PART * m + PART)
                        mm = three(UP_BANK[m % 2][:, :], (w_hi[:, UP, c, cols], w_lo[:, UP, c, cols]),
                                   (xT_hi[:, c, :], xT_lo[:, c, :]), c == 0, c == KC - 1)
                    mm.then_inc(up_mm, 1)
                for t in range(NT):
                    for c in range(KC):
                        rows = slice(PART * t, PART * t + PART)
                        mm = three(GATE_BANK[:, NE * t:NE * t + NE], (xT_hi[:, c, rows], xT_lo[:, c, rows]),
                                   (sh.g_hi[:, c, :], sh.g_lo[:, c, :]), c == 0, c == KC - 1)
                mm.then_inc(gate_mm, 1)
                for t in range(NT):
                    rows = slice(PART * t, PART * t + PART)
                    if t >= 2:
                        pe.wait_ge(y_done, NT * b + t - 1)
                    for c in range(KC):
                        mm = three(EXP_BANK[t % 2][:, :], (xT_hi[:, c, rows], xT_lo[:, c, rows]),
                                   (w_hi[:, EXPERT, c, :], w_lo[:, EXPERT, c, :]), c == 0, c == KC - 1)
                    mm.then_inc(exp_mm, 1)
                    if t == 0:
                        pe.wait_ge(h_lo_done, KC * (b + 1))
                    for c in range(KC):
                        mm = three(DOWN_BANK[t % 2][:, :], (h_hi[:, c, rows], h_lo[:, c, rows]),
                                   (w_hi[:, DOWN, c, :], w_lo[:, DOWN, c, :]), c == 0, c == KC - 1)
                    mm.then_inc(down_mm, 1)
                pe.wait_ge(y_done, NT * (b + 1) - 1)

        @block.vector
        def _(dve):
            def ln_stats(b):
                dve.wait_ge(x_loaded, 16 * (b + 1))
                for t in range(NT):
                    nc.vector.bn_stats(stats[:, t, :], xt[:, t, :]).then_inc(ln_stat, 1)
                for t in range(NT):
                    wait_alone(dve, ln_stat, NT * b + t + 1, dve_passed)
                    nc.vector.bn_aggr(mv[:, t, :], stats[:, t, :]).then_inc(ln_mv, 1)

            def ln_norm(b):
                dve.wait_ge(ln_rstd, b + 1)
                for t in range(NT):
                    nc.vector.tensor_scalar(xln[:, t, :], xt[:, t, :], mv[:, t, 0:1], rstd[:, t:t + 1],
                                            ALU.subtract, ALU.mult).then_inc(ln_done, 1)

            ln_stats(0)
            ln_norm(0)

            def batch(b, last):
                for c in range(KC):
                    dve.wait_ge(lnt_hi, KC * b + c + 1)
                    nc.vector.tensor_tensor(xT_lo[:, c, :], T_BANK[c % 2][:, :], f32(xT_hi[:, c, :]), ALU.subtract)\
                        .then_inc(lnt_lo, 1)
                if not last:
                    ln_stats(b + 1)
                for m in range(KC):
                    dve.wait_ge(h_hi_done, KC * b + m + 1)
                    nc.vector.scalar_tensor_tensor(out=h_lo[:, m, :], in0=UP_BANK[m % 2][:, :], scalar=0.0,
                                                   in1=f32(h_hi[:, m, :]), op0=ALU.max, op1=ALU.subtract)\
                        .then_inc(h_lo_done, 1)
                if not last:
                    ln_norm(b + 1)
                done = GSTEPS * b
                dve.wait_ge(gate_mm, b + 1)
                nc.vector.tensor_copy(logits[:, :, :], GATE_BANK[:, 0:NT * NE].rearrange("p (t e) -> p t e", t=NT))\
                    .then_inc(gate_out, 1)
                wait_alone(dve, gate_out, b + 1, dve_passed)
                for t in range(NT):
                    nc.vector.max(top[:, t, :], logits[:, t, :]).then_inc(g_step, 1)
                dve.wait_ge(g_step, done + NT)
                nc.vector.tensor_tensor(gap[:, :], top[:, :, 1], top[:, :, 0], ALU.subtract).then_inc(g_step, 1)
                dve.wait_ge(e2_done, b + 1)
                nc.vector.tensor_scalar(den[:, :], e2[:, :], 1.0, None, ALU.add).then_inc(g_step, 1)
                dve.wait_ge(g_step, done + NT + 2)
                nc.vector.reciprocal(rw1[:, :], den[:, :]).then_inc(g_step, 1)
                dve.wait_ge(g_step, done + NT + 3)
                nc.vector.tensor_tensor(rw2[:, :], e2[:, :], rw1[:, :], ALU.mult).then_inc(g_step, 1)
                dve.wait_ge(g_step, done + NT + 4)
                nc.vector.tensor_tensor(rw[:, :], rw1[:, :], rw2[:, :], ALU.add).then_inc(g_step, 1)
                dve.wait_ge(g_step, done + NT + 5)
                dve.wait_ge(res_loaded, 16 * (b + 1))
                for t in range(NT):
                    dve.wait_ge(exp_mm, NT * b + t + 1)
                    nc.vector.scalar_tensor_tensor(out=xres[:, t, :], in0=EXP_BANK[t % 2][:, :],
                                                   scalar=rw[:, t:t + 1], in1=xres[:, t, :], op0=ALU.mult,
                                                   op1=ALU.add).then_inc(y_mid, 1)
                    dve.wait_ge(down_mm, NT * b + t + 1)
                    dve.wait_ge(y_mid, NT * b + t + 1)
                    nc.vector.tensor_tensor(xres[:, t, :], DOWN_BANK[t % 2][:, :], xres[:, t, :], ALU.add)\
                        .then_inc(y_done, 1)

            with dve.Fori(0, B - 1) as b:
                batch(b, False)
            batch(B - 1, True)

        @block.scalar
        def _(act):
            with act.Fori(0, B) as b:
                for c in range(KC):
                    act.wait_ge(lnt_mm, KC * b + c + 1)
                    nc.scalar.activation(xT_hi[:, c, :], T_BANK[c % 2][:, :], ACT.Copy).then_inc(lnt_hi, 1)
                for m in range(KC):
                    act.wait_ge(up_mm, KC * b + m + 1)
                    nc.scalar.activation(h_hi[:, m, :], UP_BANK[m % 2][:, :], ACT.Relu).then_inc(h_hi_done, 1)
                act.wait_ge(g_step, GSTEPS * b + NT + 1)
                nc.scalar.activation(e2[:, :], gap[:, :], ACT.Exp).then_inc(e2_done, 1)

        @block.gpsimd
        def _(pool):
            with pool.Fori(0, B) as b:
                wait_alone(pool, ln_mv, NT * (b + 1), pool_passed)
                nc.gpsimd.tensor_scalar(veps[:, :], mv[:, :, 1], EPS, None, ALU.add).then_inc(ln_eps, 1)
                pool.wait_ge(ln_eps, b + 1)
                nc.gpsimd.tensor_tensor(rstd[:, :], veps[:, :], sh.neg_half[:, 0:NT], ALU.pow).then_inc(ln_rstd, 1)


def constants(nc, sh):
    with ExitStack() as ctx:
        g_raw = ctx.enter_context(nc.sbuf_tensor("g_raw", [PART, KC, NE], F32))
        made, small_in, g_split = (ctx.enter_context(nc.semaphore(n)) for n in ("made", "small_in", "g_split"))
        block = ctx.enter_context(nc.Block())

        @block.sync
        def _(sp):
            sp.dma_start(sh.qkb[:, 0, :], sh.dram["q_b"]).then_inc(small_in, 16)
            sp.dma_start(sh.qkb[:, 1, :], sh.dram["k_b"]).then_inc(small_in, 16)
            for name, tile in (("v_b", sh.v_bias), ("o_b", sh.o_bias)):
                sp.dma_start(tile[:, :], sh.dram[name].broadcast_to([PART, D])).then_inc(small_in, 16)
            sp.dma_start(g_raw[:, :, :], sh.dram["gT"].rearrange("(c p) e -> p c e", p=PART)).then_inc(small_in, 16)

        @block.gpsimd
        def _(pool):
            nc.gpsimd.memset(sh.ident[:, :], 0.0).then_inc(made, 1)
            nc.gpsimd.memset(sh.mask[:, :], 0.0).then_inc(made, 1)
            nc.gpsimd.memset(sh.ones[:, :], 1.0).then_inc(made, 1)
            nc.gpsimd.memset(sh.neg_half[:, :], -0.5).then_inc(made, 1)
            pool.wait_ge(made, 4)
            nc.gpsimd.affine_select(out=sh.ident[:, :], in_=sh.ident[:, :], compare_op=ALU.not_equal, fill=1.0,
                                    base=0, pattern=[[-1, PART]], channel_multiplier=1).then_inc(made, 1)
            d = sh.mask[:, T - PART:T]
            nc.gpsimd.affine_select(out=d, in_=d, compare_op=ALU.is_ge, fill=MASKED, base=0,
                                    pattern=[[-1, PART]], channel_multiplier=1).then_inc(made, 1)

        @block.vector
        def _(dve):
            dve.wait_ge(made, 6)
            nc.vector.tensor_copy(sh.ident_r[:, :], sh.ident[:, :]).then_inc(g_split, 1)
            dve.wait_ge(small_in, 16 * 5)
            nc.vector.tensor_copy(sh.g_hi[:, :, :], g_raw[:, :, :]).then_inc(g_split, 1)
            dve.wait_ge(g_split, 2)
            nc.vector.tensor_tensor(sh.g_lo[:, :, :], g_raw[:, :, :], f32(sh.g_hi[:, :, :]), ALU.subtract)\
                .then_inc(g_split, 1)
            dve.wait_ge(g_split, 3)


def decoder_block(nc, dram):
    sh = Shared()
    sh.dram = dram
    with ExitStack() as ctx:
        def sb(name, shape, dt=F32):
            return ctx.enter_context(nc.sbuf_tensor(name, shape, dt))

        sh.w_hi = sb("w_hi", [PART, 4, KC, D], F32R)
        sh.w_lo = sb("w_lo", [PART, 4, KC, D], F32R)
        sh.g_hi = sb("g_hi", [PART, KC, NE], F32R)
        sh.g_lo = sb("g_lo", [PART, KC, NE], F32R)
        sh.ident = sb("ident", [PART, PART])
        sh.ident_r = sb("ident_r", [PART, PART], F32R)
        sh.ones = sb("ones", [PART, HD])
        sh.neg_half = sb("neg_half", [PART, NT])
        sh.mask = sb("mask", [PART, T])
        sh.qkb = sb("qkb", [PART, 2, KC])
        sh.v_bias = sb("v_bias", [PART, D])
        sh.o_bias = sb("o_bias", [PART, D])

        constants(nc, sh)
        split_weight(nc, sh, "attn", ["qT", "kT", "vT", "oT"], range(4))
        attention(nc, sh, cross=False)
        split_weight(nc, sh, "ffn", ["upT", "downT", "expert"], range(3))
        attention(nc, sh, cross=True)
        ffn(nc, sh)


def kernel(**inputs):
    import numpy as _np
    import concourse.bacc as _bacc
    from concourse.bass_utils import run_bass_kernel_spmd as _run

    nc = _bacc.Bacc("TRN2", target_bir_lowering=False, num_devices=1)
    a = {k: _np.asarray(v) for k, v in inputs.items()}
    rows = B * T

    def column(v):
        return v.reshape(KC, PART).T

    laid = {
        "x": a["x"].reshape(rows, D),
        "ctx": a["ctx_2048"].reshape(rows, D),
        "ctxT": a["ctx_2048"].transpose(0, 2, 1).reshape(B * D, T),
        "qT": a["L0_attn_q_w"].T, "kT": a["L0_attn_k_w"].T, "vT": a["L0_attn_v_w"].T, "oT": a["L0_attn_o_w"].T,
        "q_b": column(a["L0_attn_q_b"]), "k_b": column(a["L0_attn_k_b"]),
        "v_b": a["L0_attn_v_b"].reshape(1, D), "o_b": a["L0_attn_o_b"].reshape(1, D),
        "upT": a["L0_ffn_W_up"].T, "downT": a["L0_ffn_W_down"].T, "expert": a["L0_ffn_W_expert"],
        "gT": a["L0_ffn_W_gate"].T,
    }
    laid = {k: _np.ascontiguousarray(v) for k, v in laid.items()}
    dram = {k: nc.dram_tensor(f"in_{k}", list(v.shape), F32, kind="ExternalInput").ap() for k, v in laid.items()}
    dram["x2"] = nc.dram_tensor("x2", [rows, D], F32, kind="Internal").ap()
    dram["x3"] = nc.dram_tensor("x3", [rows, D], F32, kind="Internal").ap()
    dram["out"] = nc.dram_tensor("out", [rows, D], F32, kind="ExternalOutput").ap()
    decoder_block(nc, dram)
    r = _run(nc, [{f"in_{k}": v for k, v in laid.items()}], core_ids=[0])
    return r.results[0]["out"].reshape(B, T, D)
```

```python
from contextlib import ExitStack

import concourse.bass as bass
from concourse import mybir

ALU = mybir.AluOpType
ACT = mybir.ActivationFunctionType
F32 = mybir.dt.float32
F32R = mybir.dt.float32r
BF16 = mybir.dt.bfloat16

B, T, D, NH = 4, 512, 512, 16
HD = D // NH
PART = 128
NT = T // PART
KC = D // PART
PAIRS = NH // 2
NE = 8
SCALE = HD ** -0.5
EPS = 1e-5
MASKED = -1.0e38
BIG = 3.0e38
RS = 3 * HD
OFF = [PART * q * (q + 1) // 2 for q in range(NT + 1)]
QL, QH, KH, KL = range(4)


def f32(ap):
    return ap.bitcast(F32)


def wait_alone(eng, sem, value, passed):
    eng.wait_ge(sem, value)
    eng.sem_inc(passed, 1)


class Shared:
    pass


def split_weight(nc, sh, block_name, names, slots):
    with ExitStack() as ctx:
        raw = ctx.enter_context(nc.sbuf_tensor(f"raw_{block_name}", [PART, len(names), KC, D], F32))
        loaded = [ctx.enter_context(nc.semaphore(f"loaded_{n}")) for n in names]
        hi_done = ctx.enter_context(nc.semaphore(f"hi_{block_name}"))
        lo_done = ctx.enter_context(nc.semaphore(f"lo_{block_name}"))
        block = ctx.enter_context(nc.Block())

        @block.sync
        def _(sp):
            for i, name in enumerate(names):
                sp.dma_start(raw[:, i], sh.dram[name].rearrange("(c p) n -> p c n", p=PART)).then_inc(loaded[i], 16)

        @block.scalar
        def _(act):
            for i, s in enumerate(slots):
                act.wait_ge(loaded[i], 16)
                nc.scalar.activation(sh.w_hi[:, s], raw[:, i], ACT.Copy).then_inc(hi_done, 1)

        @block.vector
        def _(dve):
            for i, s in enumerate(slots):
                dve.wait_ge(hi_done, i + 1)
                nc.vector.tensor_tensor(sh.w_lo[:, s], raw[:, i], f32(sh.w_hi[:, s]), ALU.subtract)\
                    .then_inc(lo_done, 1)
            dve.wait_ge(lo_done, len(slots))


def attention(nc, sh, cross):
    tag = "x" if cross else "s"
    x_in, x_out = (sh.dram["x2"], sh.dram["x3"]) if cross else (sh.dram["x"], sh.dram["x2"])
    x_in = x_in.rearrange("(b t p) n -> b p t n", b=B, p=PART)
    x_out = x_out.rearrange("(b t p) n -> b p t n", b=B, p=PART)
    w_hi, w_lo = sh.w_hi, sh.w_lo
    WQ, WK, WV, WO = range(4)

    with ExitStack() as ctx:
        def sb(name, shape, dt=F32):
            return ctx.enter_context(nc.sbuf_tensor(f"{tag}_{name}", shape, dt))

        def sem(name):
            return ctx.enter_context(nc.semaphore(f"{tag}_{name}"))

        xt = sb("xt", [PART, NT, D])
        xln = sb("xln", [PART, NT, D]) if cross else xt
        xres = sb("xres", [PART, NT, D])
        stage = sb("stage", [PART, 2, 4, T], F32R)
        stack = sb("stack", [PART, 2, 2, 2, T], F32R)
        V = sb("V", [PART, NT, D])
        probs = sb("probs", [PART, 2, 2, OFF[NT]])
        prob = [sb(f"prob{kb}", [PART, 4, T - PART * kb]) for kb in range(NT)]
        negmax = sb("negmax", [PART, 2, 2, NT])
        rowsum = sb("rowsum", [PART, 2, 2, NT])
        rsum = sb("rsum", [PART, 2, 2, NT])
        stats = sb("stats", [PART, NT, 6])
        mv = sb("mv", [PART, NT, 2])
        veps = sb("veps", [PART, NT])
        rstd = sb("rstd", [PART, NT])
        if cross:
            kraw = sb("kraw", [PART, 2, T])
            cn = sb("cn", [PART, T])
        else:
            xT_hi = sb("xT_hi", [PART, KC, T], F32R)
            xT_lo = sb("xT_lo", [PART, KC, T], F32R)
            cx_hi = sb("cx_hi", [PART, KC, T], F32R)
            cx_lo = sb("cx_lo", [PART, KC, T], F32R)

        def bank(name):
            return ctx.enter_context(nc.psum_tensor(f"{tag}_{name}", [PART, T], F32))

        s_bank, t_bank, pv_bank, m_bank = ([bank(f"{n}{i}") for i in range(2)] for n in ("s", "t", "pv", "m"))

        x_loaded = sem("x_loaded")
        res_loaded = sem("res_loaded")
        res_biased = sem("res_biased")
        stored = sem("stored")
        v_loaded = sem("v_loaded")
        kraw_in = [sem("kraw_in0"), sem("kraw_in1")]
        stack_in = [[sem(f"stack_in{i}{h}") for h in range(2)] for i in range(2)]
        dve_passed, pool_passed, sp_passed = sem("dve_passed"), sem("pool_passed"), sem("sp_passed")
        ln_stat = sem("ln_stat")
        ln_mv = sem("ln_mv")
        ln_eps = sem("ln_eps")
        ln_rstd = sem("ln_rstd")
        ln_done = sem("ln_done")
        lnt_mm = sem("lnt_mm")
        lnt_hi = sem("lnt_hi")
        lnt_lo = sem("lnt_lo")
        q_mm, k_mm = sem("q_mm"), sem("k_mm")
        q_hi, k_hi = sem("q_hi"), sem("k_hi")
        q_lo, k_lo = sem("q_lo"), sem("k_lo")
        s_mm = sem("s_mm")
        s_max = sem("s_max")
        p_exp = sem("p_exp")
        r_done = sem("r_done")
        p_done = sem("p_done")
        t_mm = sem("t_mm")
        t_act, t_dve = sem("t_act"), sem("t_dve")
        pv_done = sem("pv_done")
        pv_out = sem("pv_out")
        cx_hi_done = sem("cx_hi_done")
        v_mm, v_out = sem("v_mm"), sem("v_out")
        o_mm, o_out = sem("o_mm"), sem("o_out")

        TD0, PV0, PO0 = NT, NT, 2
        O0 = 1 if cross else NT

        block = ctx.enter_context(nc.Block())

        def first(n, limit):
            return isinstance(n, int) and n < limit

        def sp_stack(sp, b, p):
            q = p + 2
            g = q // 2
            sp.wait_ge(q_lo, KC * b + g + 1)
            sp.wait_ge(k_lo, KC * b + g + 1)
            for h in range(2):
                if not first(PAIRS * b + p, 0):
                    sp.wait_ge(s_mm, PAIRS * (PAIRS * b + p) + NT * (h + 1))
                j = 2 * (q % 2) + h
                src = stage[HD * j:HD * j + HD, g % 2]
                for r, pick in enumerate((slice(QH, KH + 1), slice(QH, KL + 1, 2), slice(QL, KH + 1, 2))):
                    sp.dma_start(f32(stack[HD * r:HD * r + HD, q % 2, h, :, :]), f32(src[:, pick, :]))\
                        .then_inc(stack_in[q % 2][h], 16)

        def sp_kraw(sp, b, g):
            if not first(KC * b + g, 2):
                sp.wait_ge(k_lo, KC * b + g - 1)
            bb, gg = b + g // KC, g % KC
            sp.dma_start(kraw[:, g % 2, :], sh.dram["ctxT"].rearrange("(b c p) n -> b p c n", b=B, p=PART)[bb, :, gg, :])\
                .then_inc(kraw_in[g % 2], 16)

        def sp_v(sp, b):
            sp.dma_start(V[:, :, :], sh.dram["ctx"].rearrange("(b t p) n -> b p t n", b=B, p=PART)[b])\
                .then_inc(v_loaded, 16)

        @block.sync
        def _(sp):
            sp.dma_start(xt[:, :, :], x_in[0]).then_inc(x_loaded, 16)
            if cross:
                sp_kraw(sp, 0, 0)
                sp_kraw(sp, 0, 1)
                sp_v(sp, 0)
            sp.dma_start(xres[:, :, :], x_in[0]).then_inc(res_loaded, 16)

            def step(b, p, stack_, kraw_):
                if cross and kraw_ and p % 2 == 0:
                    sp_kraw(sp, b, p // 2 + 3)
                if stack_:
                    sp_stack(sp, b, p)

            for p in range(-2, 2):
                step(0, p, True, True)

            def store(b):
                wait_alone(sp, o_out, O0 + (KC if cross else NT) * (b + 1), sp_passed)
                sp.dma_start(x_out[b], xres[:, :, :]).then_inc(stored, 16)
                sp.wait_ge(stored, 16 * (b + 1))

            def batch(b, last):
                if not last:
                    sp.wait_ge(ln_done if cross else lnt_mm, KC * (b + 1))
                    sp.dma_start(xt[:, :, :], x_in[b + 1]).then_inc(x_loaded, 16)
                for p in range(2, PAIRS):
                    step(b, p, p < 6 or not last, not last)
                if last:
                    return
                step(b + 1, 0, True, True)
                if cross:
                    sp.wait_ge(pv_done, PV0 + NT * KC * (b + 1))
                    sp_v(sp, b + 1)
                step(b + 1, 1, True, True)
                store(b)
                sp.dma_start(xres[:, :, :], x_in[b + 1]).then_inc(res_loaded, 16)

            with sp.Fori(0, B - 1) as b:
                batch(b, False)
            batch(B - 1, True)
            store(B - 1)

        def mm3(out, lhs, rhs, first_, last):
            (lh, ll), (rh, rl) = lhs, rhs
            nc.tensor.matmul(out, ll, rh, start=first_, stop=False)
            nc.tensor.matmul(out, lh, rl, start=False, stop=False)
            return nc.tensor.matmul(out, lh, rh, start=False, stop=last)

        def pe_s(pe, b, p, i):
            h, qb = divmod(i, NT)
            n = PAIRS * (PAIRS * b + p) + i
            if qb == 0:
                pe.wait_ge(stack_in[p % 2][h], 48 * (NT * b + p // 2 + 1))
            if not first(n, 2):
                pe.wait_ge(s_max, n - 1)
            N = PART * (qb + 1)
            nc.tensor.matmul(s_bank[i % 2][:, 0:N], stack[0:RS, p % 2, h, 0, PART * qb:PART * qb + PART],
                             stack[0:RS, p % 2, h, 1, 0:N], start=True, stop=True).then_inc(s_mm, 1)

        def pe_t(pe, b, p, i):
            h, kb = divmod(i, NT)
            P = PAIRS * b + p
            if kb == 0:
                pe.wait_ge(p_done, PAIRS * P + NT * (h + 1))
            if kb < 2:
                pe.wait_ge(t_dve, TD0 + NT * P + 2 * h - 2 + kb + 1)
            else:
                pe.wait_ge(t_act, NT * P + 2 * h + kb - 1)
            for qb in range(kb, NT):
                mm = nc.tensor.transpose(t_bank[i % 2][:, PART * (qb - kb):PART * (qb - kb) + PART],
                                         probs[:, p % 2, h, OFF[qb] + PART * kb:OFF[qb] + PART * kb + PART],
                                         sh.ident[:, :])
            mm.then_inc(t_mm, 1)

        def pe_pv(pe, b, g, kb):
            G = KC * b + g
            P = 2 * G + 1
            if kb == 0:
                pe.wait_ge(pv_out, PO0 + G - 1)
                pe.wait_ge(v_loaded if cross else v_out, (16 if cross else NT) * (b + 1))
            pe.wait_ge(*((t_act, NT * P + 3 + kb) if kb < 2 else (t_dve, TD0 + NT * P + 1 + kb)))
            for j in range(4):
                col = PART * (g % KC) + HD * j
                mm = nc.tensor.matmul(pv_bank[g % 2][HD * j:HD * j + HD, PART * kb:T], V[:, kb, col:col + HD],
                                      prob[kb][:, j, :], start=(kb == 0), stop=(kb == NT - 1))
            mm.then_inc(pv_done, 1)

        def pe_qk(pe, b, p, part, rows_before):
            g, half = (p + 4) // 2, p % 2
            G = KC * b + g
            if cross:
                if half == 0 and part == 4:
                    if not first(G, 1):
                        pe.wait_ge(q_lo, G)
                    if g % KC == 0:
                        pe.wait_ge(ln_done, NT * (b + g // KC + 1))
                    for t in range(NT):
                        mm = nc.tensor.transpose(m_bank[0][:, PART * t:PART * t + PART],
                                                 xln[:, t, PART * (g % KC):PART * (g % KC) + PART], sh.ident[:, :])
                    mm.then_inc(q_mm, 1)
                return
            if part == 0:
                if not first(G, 1):
                    pe.wait_ge(k_lo if half else q_lo, G)
                if g % KC == 0 and half == 0:
                    pe.wait_ge(lnt_lo, KC * (b + g // KC + 1))
                if rows_before is not None:
                    pe.wait_ge(*rows_before)
            w = WK if half else WQ
            for n in (2 * part, 2 * part + 1):
                c, term = divmod(n, 3)
                cols = slice(PART * (g % KC), PART * (g % KC) + PART)
                wh, wl, xh, xl = w_hi[:, w, c, cols], w_lo[:, w, c, cols], xT_hi[:, c, :], xT_lo[:, c, :]
                lhs, rhs = ((wl, xh), (wh, xl), (wh, xh))[term]
                mm = nc.tensor.matmul(m_bank[half][:, :], lhs, rhs, start=(n == 0), stop=(n == 11))
            if part == 5:
                mm.then_inc(k_mm if half else q_mm, 1)

        def pe_lnt(pe, b):
            for c in range(KC):
                if c == 0:
                    pe.wait_ge(ln_done, NT * (b + 1))
                if c < 2 and not first(b, 1):
                    pe.wait_ge((q_lo, k_lo)[c], KC * b)
                if c >= 2:
                    pe.wait_ge(lnt_lo, KC * b + c - 1)
                for t in range(NT):
                    mm = nc.tensor.transpose(m_bank[c % 2][:, PART * t:PART * t + PART],
                                             xln[:, t, PART * c:PART * c + PART], sh.ident[:, :])
                mm.then_inc(lnt_mm, 1)

        def pe_row(out, lhs, w, t):
            rows = slice(PART * t, PART * t + PART)
            for c in range(KC):
                mm = mm3(out[:, :], (lhs[0][:, c, rows], lhs[1][:, c, rows]), (w_hi[:, w, c, :], w_lo[:, w, c, :]),
                         c == 0, c == KC - 1)
            return mm

        def pe_v(pe, b, p, t):
            if t == 0:
                pe.wait_ge(k_lo, KC * b + (p + 3) // 2 + 1)
            else:
                pe.wait_ge(v_out, NT * b + t)
            pe_row(m_bank[1], (xT_hi, xT_lo), WV, t).then_inc(v_mm, 1)

        def pe_o(pe, b, t, last):
            if t == 0:
                pe.wait_ge(pv_out, PO0 + KC * (b + 1))
                if not last:
                    pe.wait_ge(q_lo, KC * (b + 1) + 3)
            else:
                pe.wait_ge(o_out, O0 + NT * b + t)
            pe_row(m_bank[0], (cx_hi, cx_lo), WO, t).then_inc(o_mm, 1)

        def pe_back(pe, b, g):
            G = KC * b + g
            pe.wait_ge(pv_out, PO0 + G + 1)
            pe.wait_ge(o_out, O0 + G)
            for t in range(NT):
                mm = nc.tensor.transpose(m_bank[1][:, PART * t:PART * t + PART], cn[:, PART * t:PART * t + PART],
                                         sh.ident[:, :])
            mm.then_inc(o_mm, 1)

        @block.tensor
        def _(pe):
            pe.sem_inc(pv_done, PV0)
            pe.sem_inc(o_mm, O0)

            def step(b, p, s_=True, t_=True, tail=True, qk_=True, v_=False, o_=False, rows_before=None):
                for i in range(PAIRS):
                    if s_:
                        pe_s(pe, b, p + 1, i)
                    if t_:
                        pe_t(pe, b, p, i)
                    if t_ and p % 2 == 1 and i >= 6:
                        pe_pv(pe, b, p // 2, i - 6)
                    if tail and p % 2 == 0 and i < 2:
                        pe_pv(pe, b, p // 2 - 1, i + 2)
                    if qk_ and 1 <= i <= 6:
                        pe_qk(pe, b, p, i - 1, rows_before)
                    if cross and tail and p % 2 == 0 and i == 6:
                        pe_back(pe, b, p // 2 - 1)
                    if v_ and not cross and i % 2 == 1:
                        pe_v(pe, b, p, i // 2)
                    if o_ and not cross and i % 2 == 1:
                        pe_o(pe, b - 1, i // 2, False)

            if not cross:
                pe_lnt(pe, 0)
            for p in range(-4, 0):
                step(0, p, s_=p == -1, t_=False, tail=False, v_=p == -2,
                     rows_before=(v_out, NT) if p == -1 else None)
            step(0, 0, tail=False)
            step(0, 1)

            def batch(b, last):
                for p in range(2, PAIRS):
                    if p == 4 and not cross and not last:
                        pe_lnt(pe, b + 1)
                    step(b, p, s_=p < 7 or not last, qk_=p < 4 or not last,
                         rows_before=(o_out, O0 + NT * b) if p == 2 and not cross else None)
                if last:
                    pe_pv(pe, b, KC - 1, 2)
                    pe_pv(pe, b, KC - 1, 3)
                    if cross:
                        pe_back(pe, b, KC - 1)
                    else:
                        for t in range(NT):
                            pe_o(pe, b, t, True)
                    return
                step(b + 1, 0, v_=True)
                step(b + 1, 1, o_=True, rows_before=None if cross else (v_out, NT * (b + 2)))

            with pe.Fori(0, B - 1) as b:
                batch(b, False)
            batch(B - 1, True)

        def dve_s(dve, b, p, i):
            h, qb = divmod(i, NT)
            n = PAIRS * (PAIRS * b + p) + i
            N = PART * (qb + 1)
            wait_alone(dve, s_mm, n + 1, dve_passed)
            nc.vector.tensor_tensor_reduce(probs[:, p % 2, h, OFF[qb]:OFF[qb + 1]], s_bank[i % 2][:, 0:N],
                                           sh.mask[:, T - N:T], -SCALE, BIG, ALU.add, ALU.min,
                                           negmax[:, p % 2, h, qb:qb + 1]).then_inc(s_max, 1)

        def dve_recip(dve, b, p, h, part):
            dve.wait_ge(p_exp, PAIRS * (PAIRS * b + p) + NT * h + 3 + part)
            qs = slice(3, 4) if part else slice(0, 3)
            nc.vector.reciprocal(rsum[:, p % 2, h, qs], rowsum[:, p % 2, h, qs]).then_inc(r_done, 1)

        def dve_t(dve, b, p, i):
            h, kb = divmod(i, NT)
            P = PAIRS * b + p
            dve.wait_ge(t_mm, PAIRS * P + i + 1)
            if p % 2 == 0 and h == 0:
                dve.wait_ge(pv_done, PV0 + NT * (KC * b + p // 2 - 1) + kb + 1)
            nc.vector.tensor_copy(prob[kb][:, 2 * (p % 2) + h, :], t_bank[i % 2][:, 0:T - PART * kb]).then_inc(t_dve, 1)

        def dve_qk(dve, b, p):
            g, half = (p + 4) // 2, p % 2
            G = KC * b + g
            if cross and half:
                return
            dve.wait_ge(k_hi if half else q_hi, G + 1)
            out = stage[:, g % 2, KL if half else QL, :]
            hi = f32(stage[:, g % 2, KH if half else QH, :])
            if cross:
                nc.vector.tensor_tensor(out, m_bank[0][:, :], hi, ALU.subtract).then_inc(q_lo, 1)
            else:
                nc.vector.scalar_tensor_tensor(out=out, in0=m_bank[half][:, :],
                                               scalar=sh.bias[:, half, g % KC:g % KC + 1],
                                               in1=hi, op0=ALU.add, op1=ALU.subtract)\
                    .then_inc(k_lo if half else q_lo, 1)

        def dve_ln_stats(dve, b, t):
            if t == 0:
                dve.wait_ge(x_loaded, 16 * (b + 1))
            nc.vector.bn_stats(stats[:, t, :], xt[:, t, :]).then_inc(ln_stat, 1)
            wait_alone(dve, ln_stat, NT * b + t + 1, dve_passed)
            nc.vector.bn_aggr(mv[:, t, :], stats[:, t, :]).then_inc(ln_mv, 1)

        def dve_ln_norm(dve, b, t):
            if t == 0:
                dve.wait_ge(ln_rstd, b + 1)
            nc.vector.tensor_scalar(xln[:, t, :], xt[:, t, :], mv[:, t, 0:1], rstd[:, t:t + 1],
                                    ALU.subtract, ALU.mult).then_inc(ln_done, 1)

        def dve_lnt(dve, b, c):
            dve.wait_ge(lnt_hi, KC * b + c + 1)
            nc.vector.tensor_tensor(xT_lo[:, c, :], m_bank[c % 2][:, :], f32(xT_hi[:, c, :]), ALU.subtract)\
                .then_inc(lnt_lo, 1)

        def dve_cx(dve, b, g):
            G = KC * b + g
            dve.wait_ge(cx_hi_done, G + 1)
            nc.vector.scalar_tensor_tensor(out=cx_lo[:, g % KC, :], in0=pv_bank[g % 2][:, :],
                                           scalar=sh.bias[:, 2, g % KC:g % KC + 1], in1=f32(cx_hi[:, g % KC, :]),
                                           op0=ALU.add, op1=ALU.subtract).then_inc(pv_out, 1)

        def dve_back(dve, b, g):
            G = KC * b + g
            dve.wait_ge(o_mm, O0 + G + 1)
            if g % KC == 0:
                dve.wait_ge(res_loaded, 16 * (b + 1))
            cols = slice(PART * (g % KC), PART * (g % KC) + PART)
            nc.vector.tensor_tensor(xres[:, :, cols], m_bank[1][:, :].rearrange("p (t n) -> p t n", t=NT),
                                    xres[:, :, cols], ALU.add).then_inc(o_out, 1)

        def dve_o(dve, b, t):
            if t == 0:
                dve.wait_ge(res_biased, NT * (b + 1))
            dve.wait_ge(o_mm, O0 + NT * b + t + 1)
            nc.vector.tensor_tensor(xres[:, t, :], m_bank[0][:, :], xres[:, t, :], ALU.add).then_inc(o_out, 1)

        @block.vector
        def _(dve):
            dve.sem_inc(t_dve, TD0)
            dve.sem_inc(o_out, O0)
            if not cross:
                dve.sem_inc(pv_out, PO0)

            def step(b, p, s_=True, t_=True, tail=True, lo_=True, o_=False, ln_=False):
                for i in range(PAIRS):
                    if s_:
                        dve_s(dve, b, p + 1, i)
                    if t_ and i % NT >= 2:
                        dve_t(dve, b, p, i)
                    if i == 0:
                        if t_:
                            dve_recip(dve, b, p, 1, 1)
                        if lo_:
                            dve_qk(dve, b, p - 1)
                        if cross and t_ and p % 2 == 1 and tail:
                            dve_back(dve, b, (p - 3) // 2)
                    if ln_ and 1 <= i <= 4:
                        dve_ln_stats(dve, b + 1, i - 1)
                    if s_ and i in (3, 4, 7):
                        h, part = {3: (0, 0), 4: (0, 1), 7: (1, 0)}[i]
                        dve_recip(dve, b, p + 1, h, part)
                    if not cross and tail and p % 2 == 0 and i == 5:
                        dve_cx(dve, b, p // 2 - 1)
                    if o_ and not cross and i % 2 == 1:
                        dve_o(dve, b - 1, i // 2)
                if ln_:
                    if cross:
                        dve.wait_ge(q_mm, KC * (b + 1))
                    for t in range(NT):
                        dve_ln_norm(dve, b + 1, t)

            for t in range(NT):
                dve_ln_stats(dve, 0, t)
            for t in range(NT):
                dve_ln_norm(dve, 0, t)
            if not cross:
                for c in range(KC):
                    dve_lnt(dve, 0, c)
            for p in range(-4, 0):
                step(0, p, s_=p == -1, t_=False, tail=False, lo_=p > -4)
            step(0, 0, tail=False)
            step(0, 1, tail=False)

            def batch(b, last):
                for p in range(2, PAIRS):
                    lnt = p == 4 and not cross and not last
                    if lnt:
                        dve_qk(dve, b, p - 1)
                        for c in range(KC):
                            dve_lnt(dve, b + 1, c)
                    step(b, p, s_=p < 7 or not last, lo_=(p < 5 or not last) and not lnt, ln_=p == 3 and not last)
                if last:
                    if cross:
                        dve_back(dve, b, KC - 1)
                    else:
                        dve_cx(dve, b, KC - 1)
                        for t in range(NT):
                            dve_o(dve, b, t)
                    return
                step(b + 1, 0)
                step(b + 1, 1, o_=True)

            with dve.Fori(0, B - 1) as b:
                batch(b, False)
            batch(B - 1, True)

        def act_exp(act, b, p, i):
            h, qb = divmod(i, NT)
            act.wait_ge(s_max, PAIRS * (PAIRS * b + p) + i + 1)
            tile = probs[:, p % 2, h, OFF[qb]:OFF[qb + 1]]
            nc.scalar.activation(tile, tile, ACT.Exp, bias=negmax[:, p % 2, h, qb:qb + 1], scale=-1.0,
                                 accum_out=rowsum[:, p % 2, h, qb:qb + 1]).then_inc(p_exp, 1)

        def act_t(act, b, p, i):
            h, kb = divmod(i, NT)
            P = PAIRS * b + p
            act.wait_ge(t_mm, PAIRS * P + i + 1)
            if p % 2 == 0 and h == 0:
                act.wait_ge(pv_done, PV0 + NT * (KC * b + p // 2 - 1) + kb + 1)
            nc.scalar.activation(prob[kb][:, 2 * (p % 2) + h, :], t_bank[i % 2][:, 0:T - PART * kb], ACT.Copy)\
                .then_inc(t_act, 1)

        def act_qk(act, b, p):
            g, half = (p + 4) // 2, p % 2
            G = KC * b + g
            out = stage[:, g % 2, KH if half else QH, :]
            if cross and half:
                act.wait_ge(kraw_in[g % 2], 16 * (2 * b + g // 2 + 1))
                nc.scalar.activation(out, kraw[:, g % 2, :], ACT.Copy).then_inc(k_hi, 1)
            elif cross:
                act.wait_ge(q_mm, G + 1)
                nc.scalar.activation(out, m_bank[0][:, :], ACT.Copy).then_inc(q_hi, 1)
            else:
                act.wait_ge(k_mm if half else q_mm, G + 1)
                nc.scalar.activation(out, m_bank[half][:, :], ACT.Identity, bias=sh.bias[:, half, g % KC:g % KC + 1])\
                    .then_inc(k_hi if half else q_hi, 1)

        def act_lnt(act, b, c):
            act.wait_ge(lnt_mm, KC * b + c + 1)
            nc.scalar.activation(xT_hi[:, c, :], m_bank[c % 2][:, :], ACT.Copy).then_inc(lnt_hi, 1)

        def act_pv(act, b, g):
            G = KC * b + g
            act.wait_ge(pv_done, PV0 + NT * (G + 1))
            if cross:
                act.wait_ge(o_mm, O0 + G)
                nc.scalar.activation(cn[:, :], pv_bank[g % 2][:, :], ACT.Copy).then_inc(pv_out, 1)
                return
            if g % KC == 0:
                act.wait_ge(o_mm, O0 + NT * b)
            nc.scalar.activation(cx_hi[:, g % KC, :], pv_bank[g % 2][:, :], ACT.Identity,
                                 bias=sh.bias[:, 2, g % KC:g % KC + 1]).then_inc(cx_hi_done, 1)

        def act_v(act, b, t):
            act.wait_ge(v_mm, NT * b + t + 1)
            act.wait_ge(pv_done, PV0 + NT * (KC * b - 1) + t + 1)
            nc.scalar.activation(V[:, t, :], m_bank[1][:, :], ACT.Copy).then_inc(v_out, 1)

        @block.scalar
        def _(act):
            if cross:
                act.sem_inc(pv_out, PO0)

            def step(b, p, s_=True, t_=True, tail=True, qk_=True, v_=False):
                for i in range(PAIRS):
                    if t_ and i % NT < 2:
                        act_t(act, b, p, i)
                    if s_:
                        act_exp(act, b, p + 1, i)
                    if tail and p % 2 == 0 and i == 3:
                        act_pv(act, b, p // 2 - 1)
                    if v_ and not cross and i % 2 == 1:
                        act_v(act, b, i // 2)
                if qk_:
                    act_qk(act, b, p)

            if not cross:
                for c in range(KC):
                    act_lnt(act, 0, c)
            for p in range(-4, 0):
                step(0, p, s_=p == -1, t_=False, tail=False, v_=p == -2)
            step(0, 0, tail=False)
            step(0, 1)

            def batch(b, last):
                for p in range(2, PAIRS):
                    if p == 4 and not cross and not last:
                        for c in range(KC):
                            act_lnt(act, b + 1, c)
                    step(b, p, s_=p < 7 or not last, qk_=p < 4 or not last)
                if last:
                    act_pv(act, b, KC - 1)
                    return
                step(b + 1, 0, v_=True)
                step(b + 1, 1)

            with act.Fori(0, B - 1) as b:
                batch(b, False)
            batch(B - 1, True)

        def pool_p(pool, b, p, i):
            h, qb = divmod(i, NT)
            wait_alone(pool, r_done, 2 * (2 * (PAIRS * b + p) + h) + 1 + qb // 3, pool_passed)
            tile = probs[:, p % 2, h, OFF[qb]:OFF[qb + 1]]
            nc.gpsimd.tensor_scalar(tile, tile, rsum[:, p % 2, h, qb:qb + 1], 0.0, ALU.mult, ALU.add)\
                .then_inc(p_done, 1)

        def pool_rstd(pool, b):
            wait_alone(pool, ln_mv, NT * (b + 1), pool_passed)
            nc.gpsimd.tensor_scalar(veps[:, :], mv[:, :, 1], EPS, None, ALU.add).then_inc(ln_eps, 1)
            pool.wait_ge(ln_eps, b + 1)
            nc.gpsimd.tensor_tensor(rstd[:, :], veps[:, :], sh.neg_half[:, 0:NT], ALU.pow).then_inc(ln_rstd, 1)

        def pool_k(pool, b, p):
            g = (p + 4) // 2
            pool.wait_ge(k_hi, KC * b + g + 1)
            nc.gpsimd.tensor_tensor(stage[:, g % 2, KL, :], kraw[:, g % 2, :], f32(stage[:, g % 2, KH, :]),
                                    ALU.subtract).then_inc(k_lo, 1)

        def pool_res(pool, b, t):
            if t == 0:
                pool.wait_ge(res_loaded, 16 * (b + 1))
            nc.gpsimd.tensor_tensor(xres[:, t, :], xres[:, t, :], sh.o_bias[:, :], ALU.add).then_inc(res_biased, 1)

        @block.gpsimd
        def _(pool):
            pool_rstd(pool, 0)

            def step(b, p, s_=True, t_=True, qk_=True, ln_=False):
                if t_:
                    pool_p(pool, b, p, PAIRS - 1)
                for i in range(PAIRS - 1):
                    if s_:
                        pool_p(pool, b, p + 1, i)
                    if ln_ and i == 4:
                        pool_rstd(pool, b + 1)
                if not cross and p >= 4:
                    pool_res(pool, b, p - 4)
                if cross and qk_ and p % 2 == 1:
                    pool_k(pool, b, p)

            for p in range(-4, 0):
                step(0, p, s_=p == -1, t_=False)
            step(0, 0)
            step(0, 1)

            def batch(b, last):
                for p in range(2, PAIRS):
                    step(b, p, s_=p < 7 or not last, qk_=p < 4 or not last, ln_=p == 3 and not last)
                if last:
                    return
                step(b + 1, 0)
                step(b + 1, 1)

            with pool.Fori(0, B - 1) as b:
                batch(b, False)
            batch(B - 1, True)


def ffn(nc, sh):
    x_in = sh.dram["x3"].rearrange("(b t p) n -> b p t n", b=B, p=PART)
    x_out = sh.dram["out"].rearrange("(b t p) n -> b p t n", b=B, p=PART)
    w_hi, w_lo = sh.w_hi, sh.w_lo
    UP, DOWN, EXPERT = range(3)
    with ExitStack() as ctx:
        def sb(name, shape, dt=F32):
            return ctx.enter_context(nc.sbuf_tensor(f"f_{name}", shape, dt))

        def sem(name):
            return ctx.enter_context(nc.semaphore(f"f_{name}"))

        xt = sb("xt", [PART, NT, D])
        xln = sb("xln", [PART, NT, D])
        xres = sb("xres", [PART, NT, D])
        xT_hi = sb("xT_hi", [PART, KC, T], F32R)
        xT_lo = sb("xT_lo", [PART, KC, T], F32R)
        h_hi = sb("h_hi", [PART, KC, T], F32R)
        h_lo = sb("h_lo", [PART, KC, T], F32R)
        stats = sb("stats", [PART, NT, 6])
        mv = sb("mv", [PART, NT, 2])
        veps = sb("veps", [PART, NT])
        rstd = sb("rstd", [PART, NT])
        logits = sb("logits", [PART, NT, NE])
        top = sb("top", [PART, NT, 8])
        gap = sb("gap", [PART, NT])
        e2 = sb("e2", [PART, NT])
        den = sb("den", [PART, NT])
        rw1 = sb("rw1", [PART, NT])
        rw2 = sb("rw2", [PART, NT])
        rw = sb("rw", [PART, NT])
        bank = [ctx.enter_context(nc.psum_tensor(f"f_b{i}", [PART, T], F32)) for i in range(8)]
        T_BANK, UP_BANK, GATE_BANK, DOWN_BANK, EXP_BANK = bank[0:2], bank[0:2], bank[2], bank[4:6], bank[6:8]

        x_loaded, res_loaded, stored = sem("x_loaded"), sem("res_loaded"), sem("stored")
        ln_stat, ln_mv, ln_eps, ln_rstd, ln_done = (sem(n) for n in ("ln_stat", "ln_mv", "ln_eps", "ln_rstd",
                                                                     "ln_done"))
        lnt_mm, lnt_hi, lnt_lo = sem("lnt_mm"), sem("lnt_hi"), sem("lnt_lo")
        up_mm, h_hi_done, h_lo_done = sem("up_mm"), sem("h_hi_done"), sem("h_lo_done")
        gate_mm, gate_out = sem("gate_mm"), sem("gate_out")
        g_step = sem("g_step")
        e2_done = sem("e2_done")
        down_mm, exp_mm, y_mid, y_done = sem("down_mm"), sem("exp_mm"), sem("y_mid"), sem("y_done")
        dve_passed, pool_passed = sem("dve_passed"), sem("pool_passed")
        GSTEPS = NT + 5

        block = ctx.enter_context(nc.Block())

        @block.sync
        def _(sp):
            sp.dma_start(xt[:, :, :], x_in[0]).then_inc(x_loaded, 16)
            sp.dma_start(xres[:, :, :], x_in[0]).then_inc(res_loaded, 16)

            def batch(b, last):
                if not last:
                    sp.wait_ge(ln_done, NT * (b + 1))
                    sp.dma_start(xt[:, :, :], x_in[b + 1]).then_inc(x_loaded, 16)
                sp.wait_ge(y_done, NT * (b + 1))
                sp.dma_start(x_out[b], xres[:, :, :]).then_inc(stored, 16)
                sp.wait_ge(stored, 16 * (b + 1))
                if not last:
                    sp.dma_start(xres[:, :, :], x_in[b + 1]).then_inc(res_loaded, 16)

            with sp.Fori(0, B - 1) as b:
                batch(b, False)
            batch(B - 1, True)

        @block.tensor
        def _(pe):
            def three(out, lhs, rhs, first, last):
                nc.tensor.matmul(out, lhs[1], rhs[0], start=first, stop=False)
                nc.tensor.matmul(out, lhs[0], rhs[1], start=False, stop=False)
                return nc.tensor.matmul(out, lhs[0], rhs[0], start=False, stop=last)

            with pe.Fori(0, B) as b:
                for c in range(KC):
                    if c == 0:
                        pe.wait_ge(ln_done, NT * (b + 1))
                    if c >= 2:
                        pe.wait_ge(lnt_lo, KC * b + c - 1)
                    for t in range(NT):
                        mm = nc.tensor.transpose(T_BANK[c % 2][:, PART * t:PART * t + PART],
                                                 xln[:, t, PART * c:PART * c + PART], sh.ident[:, :])
                    mm.then_inc(lnt_mm, 1)
                pe.wait_ge(lnt_lo, KC * (b + 1))
                for m in range(KC):
                    if m >= 2:
                        pe.wait_ge(h_lo_done, KC * b + m - 1)
                    for c in range(KC):
                        cols = slice(PART * m, PART * m + PART)
                        mm = three(UP_BANK[m % 2][:, :], (w_hi[:, UP, c, cols], w_lo[:, UP, c, cols]),
                                   (xT_hi[:, c, :], xT_lo[:, c, :]), c == 0, c == KC - 1)
                    mm.then_inc(up_mm, 1)
                for t in range(NT):
                    for c in range(KC):
                        rows = slice(PART * t, PART * t + PART)
                        mm = three(GATE_BANK[:, NE * t:NE * t + NE], (xT_hi[:, c, rows], xT_lo[:, c, rows]),
                                   (sh.g_hi[:, c, :], sh.g_lo[:, c, :]), c == 0, c == KC - 1)
                mm.then_inc(gate_mm, 1)
                for t in range(NT):
                    rows = slice(PART * t, PART * t + PART)
                    if t >= 2:
                        pe.wait_ge(y_done, NT * b + t - 1)
                    for c in range(KC):
                        mm = three(EXP_BANK[t % 2][:, :], (xT_hi[:, c, rows], xT_lo[:, c, rows]),
                                   (w_hi[:, EXPERT, c, :], w_lo[:, EXPERT, c, :]), c == 0, c == KC - 1)
                    mm.then_inc(exp_mm, 1)
                    if t == 0:
                        pe.wait_ge(h_lo_done, KC * (b + 1))
                    for c in range(KC):
                        mm = three(DOWN_BANK[t % 2][:, :], (h_hi[:, c, rows], h_lo[:, c, rows]),
                                   (w_hi[:, DOWN, c, :], w_lo[:, DOWN, c, :]), c == 0, c == KC - 1)
                    mm.then_inc(down_mm, 1)
                pe.wait_ge(y_done, NT * (b + 1) - 1)

        @block.vector
        def _(dve):
            def ln_stats(b):
                dve.wait_ge(x_loaded, 16 * (b + 1))
                for t in range(NT):
                    nc.vector.bn_stats(stats[:, t, :], xt[:, t, :]).then_inc(ln_stat, 1)
                for t in range(NT):
                    wait_alone(dve, ln_stat, NT * b + t + 1, dve_passed)
                    nc.vector.bn_aggr(mv[:, t, :], stats[:, t, :]).then_inc(ln_mv, 1)

            def ln_norm(b):
                dve.wait_ge(ln_rstd, b + 1)
                for t in range(NT):
                    nc.vector.tensor_scalar(xln[:, t, :], xt[:, t, :], mv[:, t, 0:1], rstd[:, t:t + 1],
                                            ALU.subtract, ALU.mult).then_inc(ln_done, 1)

            ln_stats(0)
            ln_norm(0)

            def batch(b, last):
                for c in range(KC):
                    dve.wait_ge(lnt_hi, KC * b + c + 1)
                    nc.vector.tensor_tensor(xT_lo[:, c, :], T_BANK[c % 2][:, :], f32(xT_hi[:, c, :]), ALU.subtract)\
                        .then_inc(lnt_lo, 1)
                if not last:
                    ln_stats(b + 1)
                for m in range(KC):
                    dve.wait_ge(h_hi_done, KC * b + m + 1)
                    nc.vector.scalar_tensor_tensor(out=h_lo[:, m, :], in0=UP_BANK[m % 2][:, :], scalar=0.0,
                                                   in1=f32(h_hi[:, m, :]), op0=ALU.max, op1=ALU.subtract)\
                        .then_inc(h_lo_done, 1)
                if not last:
                    ln_norm(b + 1)
                done = GSTEPS * b
                dve.wait_ge(gate_mm, b + 1)
                nc.vector.tensor_copy(logits[:, :, :], GATE_BANK[:, 0:NT * NE].rearrange("p (t e) -> p t e", t=NT))\
                    .then_inc(gate_out, 1)
                wait_alone(dve, gate_out, b + 1, dve_passed)
                for t in range(NT):
                    nc.vector.max(top[:, t, :], logits[:, t, :]).then_inc(g_step, 1)
                dve.wait_ge(g_step, done + NT)
                nc.vector.tensor_tensor(gap[:, :], top[:, :, 1], top[:, :, 0], ALU.subtract).then_inc(g_step, 1)
                dve.wait_ge(e2_done, b + 1)
                nc.vector.tensor_scalar(den[:, :], e2[:, :], 1.0, None, ALU.add).then_inc(g_step, 1)
                dve.wait_ge(g_step, done + NT + 2)
                nc.vector.reciprocal(rw1[:, :], den[:, :]).then_inc(g_step, 1)
                dve.wait_ge(g_step, done + NT + 3)
                nc.vector.tensor_tensor(rw2[:, :], e2[:, :], rw1[:, :], ALU.mult).then_inc(g_step, 1)
                dve.wait_ge(g_step, done + NT + 4)
                nc.vector.tensor_tensor(rw[:, :], rw1[:, :], rw2[:, :], ALU.add).then_inc(g_step, 1)
                dve.wait_ge(g_step, done + NT + 5)
                dve.wait_ge(res_loaded, 16 * (b + 1))
                for t in range(NT):
                    dve.wait_ge(exp_mm, NT * b + t + 1)
                    nc.vector.scalar_tensor_tensor(out=xres[:, t, :], in0=EXP_BANK[t % 2][:, :],
                                                   scalar=rw[:, t:t + 1], in1=xres[:, t, :], op0=ALU.mult,
                                                   op1=ALU.add).then_inc(y_mid, 1)
                    dve.wait_ge(down_mm, NT * b + t + 1)
                    dve.wait_ge(y_mid, NT * b + t + 1)
                    nc.vector.tensor_tensor(xres[:, t, :], DOWN_BANK[t % 2][:, :], xres[:, t, :], ALU.add)\
                        .then_inc(y_done, 1)

            with dve.Fori(0, B - 1) as b:
                batch(b, False)
            batch(B - 1, True)

        @block.scalar
        def _(act):
            with act.Fori(0, B) as b:
                for c in range(KC):
                    act.wait_ge(lnt_mm, KC * b + c + 1)
                    nc.scalar.activation(xT_hi[:, c, :], T_BANK[c % 2][:, :], ACT.Copy).then_inc(lnt_hi, 1)
                for m in range(KC):
                    act.wait_ge(up_mm, KC * b + m + 1)
                    nc.scalar.activation(h_hi[:, m, :], UP_BANK[m % 2][:, :], ACT.Relu).then_inc(h_hi_done, 1)
                act.wait_ge(g_step, GSTEPS * b + NT + 1)
                nc.scalar.activation(e2[:, :], gap[:, :], ACT.Exp).then_inc(e2_done, 1)

        @block.gpsimd
        def _(pool):
            with pool.Fori(0, B) as b:
                wait_alone(pool, ln_mv, NT * (b + 1), pool_passed)
                nc.gpsimd.tensor_scalar(veps[:, :], mv[:, :, 1], EPS, None, ALU.add).then_inc(ln_eps, 1)
                pool.wait_ge(ln_eps, b + 1)
                nc.gpsimd.tensor_tensor(rstd[:, :], veps[:, :], sh.neg_half[:, 0:NT], ALU.pow).then_inc(ln_rstd, 1)


def constants(nc, sh):
    with ExitStack() as ctx:
        g_raw = ctx.enter_context(nc.sbuf_tensor("g_raw", [PART, KC, NE], F32))
        made, small_in, g_split = (ctx.enter_context(nc.semaphore(n)) for n in ("made", "small_in", "g_split"))
        block = ctx.enter_context(nc.Block())

        @block.sync
        def _(sp):
            for i, name in enumerate(("q_b", "k_b", "v_b")):
                sp.dma_start(sh.bias[:, i, :], sh.dram[name]).then_inc(small_in, 16)
            sp.dma_start(sh.o_bias[:, :], sh.dram["o_b"].broadcast_to([PART, D])).then_inc(small_in, 16)
            sp.dma_start(g_raw[:, :, :], sh.dram["gT"].rearrange("(c p) e -> p c e", p=PART)).then_inc(small_in, 16)

        @block.gpsimd
        def _(pool):
            nc.gpsimd.memset(sh.ident[:, :], 0.0).then_inc(made, 1)
            nc.gpsimd.memset(sh.mask[:, :], 0.0).then_inc(made, 1)
            nc.gpsimd.memset(sh.neg_half[:, :], -0.5).then_inc(made, 1)
            pool.wait_ge(made, 3)
            nc.gpsimd.affine_select(out=sh.ident[:, :], in_=sh.ident[:, :], compare_op=ALU.not_equal, fill=1.0,
                                    base=0, pattern=[[-1, PART]], channel_multiplier=1).then_inc(made, 1)
            d = sh.mask[:, T - PART:T]
            nc.gpsimd.affine_select(out=d, in_=d, compare_op=ALU.is_ge, fill=MASKED, base=0,
                                    pattern=[[-1, PART]], channel_multiplier=1).then_inc(made, 1)

        @block.vector
        def _(dve):
            dve.wait_ge(small_in, 16 * 5)
            nc.vector.tensor_copy(sh.g_hi[:, :, :], g_raw[:, :, :]).then_inc(g_split, 1)
            dve.wait_ge(g_split, 1)
            nc.vector.tensor_tensor(sh.g_lo[:, :, :], g_raw[:, :, :], f32(sh.g_hi[:, :, :]), ALU.subtract)\
                .then_inc(g_split, 1)
            dve.wait_ge(g_split, 2)


def decoder_block(nc, dram):
    sh = Shared()
    sh.dram = dram
    with ExitStack() as ctx:
        def sb(name, shape, dt=F32):
            return ctx.enter_context(nc.sbuf_tensor(name, shape, dt))

        sh.w_hi = sb("w_hi", [PART, 4, KC, D], F32R)
        sh.w_lo = sb("w_lo", [PART, 4, KC, D], F32R)
        sh.g_hi = sb("g_hi", [PART, KC, NE], F32R)
        sh.g_lo = sb("g_lo", [PART, KC, NE], F32R)
        sh.ident = sb("ident", [PART, PART])
        sh.neg_half = sb("neg_half", [PART, NT])
        sh.mask = sb("mask", [PART, T])
        sh.bias = sb("bias", [PART, 3, KC])
        sh.o_bias = sb("o_bias", [PART, D])

        constants(nc, sh)
        split_weight(nc, sh, "attn", ["qT", "kT", "vT", "oT"], range(4))
        attention(nc, sh, cross=False)
        split_weight(nc, sh, "ffn", ["upT", "downT", "expert"], range(3))
        attention(nc, sh, cross=True)
        ffn(nc, sh)


def kernel(**inputs):
    import numpy as _np
    import concourse.bacc as _bacc
    from concourse.bass_utils import run_bass_kernel_spmd as _run

    nc = _bacc.Bacc("TRN2", target_bir_lowering=False, num_devices=1)
    a = {k: _np.asarray(v) for k, v in inputs.items()}
    rows = B * T

    def column(v):
        return v.reshape(KC, PART).T

    laid = {
        "x": a["x"].reshape(rows, D),
        "ctx": a["ctx_2048"].reshape(rows, D),
        "ctxT": a["ctx_2048"].transpose(0, 2, 1).reshape(B * D, T),
        "qT": a["L0_attn_q_w"].T, "kT": a["L0_attn_k_w"].T, "vT": a["L0_attn_v_w"].T, "oT": a["L0_attn_o_w"].T,
        "q_b": column(a["L0_attn_q_b"]), "k_b": column(a["L0_attn_k_b"]),
        "v_b": column(a["L0_attn_v_b"]), "o_b": a["L0_attn_o_b"].reshape(1, D),
        "upT": a["L0_ffn_W_up"].T, "downT": a["L0_ffn_W_down"].T, "expert": a["L0_ffn_W_expert"],
        "gT": a["L0_ffn_W_gate"].T,
    }
    laid = {k: _np.ascontiguousarray(v) for k, v in laid.items()}
    dram = {k: nc.dram_tensor(f"in_{k}", list(v.shape), F32, kind="ExternalInput").ap() for k, v in laid.items()}
    dram["x2"] = nc.dram_tensor("x2", [rows, D], F32, kind="Internal").ap()
    dram["x3"] = nc.dram_tensor("x3", [rows, D], F32, kind="Internal").ap()
    dram["out"] = nc.dram_tensor("out", [rows, D], F32, kind="ExternalOutput").ap()
    decoder_block(nc, dram)
    r = _run(nc, [{f"in_{k}": v for k, v in laid.items()}], core_ids=[0])
    return r.results[0]["out"].reshape(B, T, D)
```

```python
from contextlib import ExitStack

import concourse.bass as bass
from concourse import mybir

ALU = mybir.AluOpType
ACT = mybir.ActivationFunctionType
F32 = mybir.dt.float32
F32R = mybir.dt.float32r

B, T, D, NH = 4, 512, 512, 16
HD = D // NH
PART = 128
NT = T // PART
KC = D // PART
PAIRS = NH // 2
NE = 8
SCALE = HD ** -0.5
EPS = 1e-5
MASKED = -1.0e38
BIG = 3.0e38
RS = 3 * HD
OFF = [PART * q * (q + 1) // 2 for q in range(NT + 1)]
T_ACT, T_DVE = (0, 1, 4, 5), (2, 3, 6, 7)
QL, QH, KH, KL = range(4)


def f32(ap):
    return ap.bitcast(F32)


def wait_alone(eng, sem, value, passed):
    eng.wait_ge(sem, value)
    eng.sem_inc(passed, 1)


class Shared:
    pass


def attention(nc, sh, cross):
    tag = "x" if cross else "s"
    x_in, x_out = (sh.dram["x2"], sh.dram["x3"]) if cross else (sh.dram["x"], sh.dram["x2"])
    x_in = x_in.rearrange("(b t p) n -> b p t n", b=B, p=PART)
    x_out = x_out.rearrange("(b t p) n -> b p t n", b=B, p=PART)
    w_hi, w_lo = sh.w_hi, sh.w_lo
    LN0 = 0 if cross else 1
    STAT_AT = {(2 if cross else 0, t + 1): t for t in range(NT)}
    NORM_STEP = 3 if cross else 1
    WQ, WK, WV, WO = range(4)

    with ExitStack() as ctx:
        def sb(name, shape, dt=F32):
            return ctx.enter_context(nc.sbuf_tensor(f"{tag}_{name}", shape, dt))

        def sem(name):
            return ctx.enter_context(nc.semaphore(f"{tag}_{name}"))

        xt, stats, mv, veps, rstd = sh.xt, sh.stats, sh.mv, sh.veps, sh.rstd
        xln = sb("xln", [PART, NT, D]) if cross else xt
        xres = sh.xres
        stage = sb("stage", [PART, 2, 4, T], F32R)
        stack = sb("stack", [PART, 2, 2, 2, T], F32R)
        V = sb("V", [PART, NT, D])
        probs = sb("probs", [PART, 2, 2, OFF[NT]])
        prob = [sb(f"prob{kb}", [PART, 4, T - PART * kb]) for kb in range(NT)]
        negmax = sb("negmax", [PART, 2, 2, NT])
        rowsum = sb("rowsum", [PART, 2, 2, NT])
        rsum = sb("rsum", [PART, 2, 2, NT])
        if cross:
            kraw = sb("kraw", [PART, 2, T])
            cn = sb("cn", [PART, T])
        else:
            xT_hi = sb("xT_hi", [PART, KC, T], F32R)
            xT_lo = sb("xT_lo", [PART, KC, T], F32R)
            cx_hi = sb("cx_hi", [PART, KC, T], F32R)
            cx_lo = sb("cx_lo", [PART, KC, T], F32R)

        if cross:
            raw = [sh.ffn_raw[:, i] for i in range(3)]
        else:
            flat = probs.rearrange("p a h n -> p (a h n)")
            raw = [tile.rearrange("p (c n) -> p c n", c=KC) for tile in
                   (flat[:, 0:KC * D], flat[:, KC * D:2 * KC * D], prob[0].rearrange("p j n -> p (j n)"),
                    xres.rearrange("p t n -> p (t n)"))]

        def bank(name):
            return ctx.enter_context(nc.psum_tensor(f"{tag}_{name}", [PART, T], F32))

        s_bank, t_bank = ([bank(f"{n}{i}") for i in range(count)] for n, count in (("s", 3 if cross else 2), ("t", 3)))
        pv_bank = bank("pv")
        m_bank = [bank(f"m{i}") for i in range(1 if cross else 2)]
        NS, NTB = len(s_bank), len(t_bank)

        x_loaded = [sem(f"x_loaded{t}") for t in range(NT)]
        w_loaded = [sem(f"w_loaded{i}") for i in range(4)]
        w_hi_done, w_lo_done = sem("w_hi_done"), sem("w_lo_done")
        small_in, made = sem("small_in"), sem("made")
        res_loaded = sem("res_loaded")
        res_biased = sem("res_biased")
        stored = sh.stored[int(cross)]
        v_loaded = sem("v_loaded")
        kraw_in = [sem("kraw_in0"), sem("kraw_in1")]
        stack_in = [[sem(f"stack_in{i}{h}") for h in range(2)] for i in range(2)]
        dve_passed, pool_passed, sp_passed = sem("dve_passed"), sem("pool_passed"), sem("sp_passed")
        ln_stat = sem("ln_stat")
        ln_mv = sem("ln_mv")
        ln_eps = sem("ln_eps")
        ln_rstd = sem("ln_rstd")
        ln_done = sem("ln_done")
        lnt_mm = sem("lnt_mm")
        lnt_hi = sem("lnt_hi")
        lnt_lo = sem("lnt_lo")
        q_mm, k_mm = sem("q_mm"), sem("k_mm")
        q_hi, k_hi = sem("q_hi"), sem("k_hi")
        q_lo, k_lo = sem("q_lo"), sem("k_lo")
        s_mm = sem("s_mm")
        s_max = sem("s_max")
        p_exp = sem("p_exp")
        r_done = sem("r_done")
        p_done = sem("p_done")
        t_mm = sem("t_mm")
        t_act, t_dve = sem("t_act"), sem("t_dve")
        pv_done = sem("pv_done")
        pv_out = sem("pv_out")
        cx_hi_done = sem("cx_hi_done")
        v_mm, v_out = sem("v_mm"), sem("v_out")
        o_mm, o_out = sem("o_mm"), sem("o_out")

        TA0, TD0, PV0, PO0 = len(T_ACT), len(T_DVE), NT, 1
        O0 = 1 if cross else NT

        block = ctx.enter_context(nc.Block())

        def copied(P, i):
            if i in T_ACT:
                return t_act, TA0 + len(T_ACT) * P + T_ACT.index(i) + 1
            return t_dve, TD0 + len(T_DVE) * P + T_DVE.index(i) + 1

        def before(i, banks):
            return i - banks if i >= banks else max(j for j in range(PAIRS) if j % banks == i) - PAIRS

        def first(n, limit):
            return isinstance(n, int) and n < limit

        def sp_stack(sp, b, p):
            q = p + 2
            g = q // 2
            sp.wait_ge(q_lo, KC * b + g + 1)
            sp.wait_ge(k_lo, KC * b + g + 1)
            for h in range(2):
                if not first(PAIRS * b + p, 0):
                    sp.wait_ge(s_mm, PAIRS * (PAIRS * b + p) + NT * (h + 1))
                j = 2 * (q % 2) + h
                src = stage[HD * j:HD * j + HD, g % 2]
                for r, pick in enumerate((slice(QH, KH + 1), slice(QH, KL + 1, 2), slice(QL, KH + 1, 2))):
                    sp.dma_start(f32(stack[HD * r:HD * r + HD, q % 2, h, :, :]), f32(src[:, pick, :]))\
                        .then_inc(stack_in[q % 2][h], 16)

        def sp_kraw(sp, b, g):
            if not first(KC * b + g, 2):
                sp.wait_ge(k_lo, KC * b + g - 1)
            bb, gg = b + g // KC, g % KC
            sp.dma_start(kraw[:, g % 2, :], sh.dram["ctxT"].rearrange("(b c p) n -> b p c n", b=B, p=PART)[bb, :, gg, :])\
                .then_inc(kraw_in[g % 2], 16)

        def sp_v(sp, b):
            sp.dma_start(V[:, :, :], sh.dram["ctx"].rearrange("(b t p) n -> b p t n", b=B, p=PART)[b])\
                .then_inc(v_loaded, 16)

        @block.sync
        def _(sp):
            def step(b, p, stack_=True, kraw_=True):
                if stack_:
                    sp_stack(sp, b, p)
                if cross and kraw_ and p % 2 == 0:
                    sp_kraw(sp, b, p // 2 + 3)

            def load(b):
                if not first(b, 1):
                    wait_alone(sp, ln_done if cross else lnt_mm, KC * b, sp_passed)
                src = x_out[0] if isinstance(b, int) and b == B else x_in[b]
                for t in range(NT):
                    sp.dma_start(xt[:, t, :], src[:, t, :]).then_inc(x_loaded[t], 16)

            def load_weight(name, slot):
                sp.dma_start(raw[slot], sh.dram[name].rearrange("(c p) n -> p c n", p=PART))\
                    .then_inc(w_loaded[slot], 16)

            def store(b):
                sp.dma_start(x_out[b], xres[:, :, :]).then_inc(stored, 16)

            if not cross:
                load(0)
            if cross:
                sp_kraw(sp, 0, 0)
                sp_kraw(sp, 0, 1)
            else:
                for i, name in enumerate(("q_b", "k_b", "v_b")):
                    sp.dma_start(sh.bias[:, i, :], sh.dram[name]).then_inc(small_in, 16)
                sp.dma_start(sh.o_bias[:, :], sh.dram["o_b"].broadcast_to([PART, D])).then_inc(small_in, 16)
                for i, name in enumerate(("qT", "kT", "vT", "oT")):
                    load_weight(name, i)
            step(0, -2)
            if cross:
                sp_v(sp, 0)
            step(0, -1)
            load(1)
            if cross:
                sp.wait_ge(sh.stored[0], 16 * B)
            else:
                sp.wait_ge(w_lo_done, 4)
            sp.dma_start(xres[:, :, :], x_in[0]).then_inc(res_loaded, 16)
            for p in range(4):
                step(0, p)
            if cross:
                for i, name in enumerate(("upT", "expert", "downT")):
                    load_weight(name, i)
                sp.dma_start(sh.g_raw[:, :, :], sh.dram["gT"].rearrange("(c p) e -> p c e", p=PART))\
                    .then_inc(small_in, 16)

            def half_turn(b, last):
                for p in range(4, PAIRS):
                    step(b, p)
                    if p == 4:
                        load(b + 2)
                step(b + 1, 0)
                if cross:
                    wait_alone(sp, pv_done, PV0 + NT * KC * (b + 1), sp_passed)
                    sp_v(sp, b + 1)
                step(b + 1, 1)
                step(b + 1, 2, kraw_=False)
                wait_alone(sp, o_out, O0 + (KC if cross else NT) * (b + 1), sp_passed)
                store(b)
                if cross and not last:
                    sp_kraw(sp, b + 1, 4)
                step(b + 1, 3)
                wait_alone(sp, stored, 16 * (b + 1), sp_passed)
                sp.dma_start(xres[:, :, :], x_in[b + 1]).then_inc(res_loaded, 16)

            with sp.Fori(0, B - 2) as b:
                half_turn(b, False)
            half_turn(B - 2, True)
            for p in range(4, 6):
                step(B - 1, p, kraw_=False)
            sp.wait_ge(o_out, O0 + (KC if cross else NT) * B)
            store(B - 1)
            if cross:
                for i in range(3):
                    sp.wait_ge(w_loaded[i], 16)
                sp.wait_ge(small_in, 16)

        def mm3(out, lhs, rhs, first_, last):
            (lh, ll), (rh, rl) = lhs, rhs
            nc.tensor.matmul(out, ll, rh, start=first_, stop=False)
            nc.tensor.matmul(out, lh, rl, start=False, stop=False)
            return nc.tensor.matmul(out, lh, rh, start=False, stop=last)

        def pe_s(pe, b, p, i):
            h, qb = divmod(i, NT)
            n = PAIRS * (PAIRS * b + p) + i
            if qb == 0:
                pe.wait_ge(stack_in[p % 2][h], 48 * (NT * b + p // 2 + 1))
            if not first(n, NS):
                pe.wait_ge(s_max, PAIRS * (PAIRS * b + p) + before(i, NS) + 1)
            N = PART * (qb + 1)
            nc.tensor.matmul(s_bank[i % NS][:, 0:N], stack[0:RS, p % 2, h, 0, PART * qb:PART * qb + PART],
                             stack[0:RS, p % 2, h, 1, 0:N], start=True, stop=True).then_inc(s_mm, 1)

        def pe_t(pe, b, p, i):
            h, kb = divmod(i, NT)
            P = PAIRS * b + p
            if kb == 0:
                pe.wait_ge(p_done, PAIRS * P + NT * (h + 1))
            j = before(i, NTB)
            pe.wait_ge(*(copied(P, j) if j >= 0 else copied(P - 1, PAIRS + j)))
            for qb in range(kb, NT):
                mm = nc.tensor.transpose(t_bank[i % NTB][:, PART * (qb - kb):PART * (qb - kb) + PART],
                                         probs[:, p % 2, h, OFF[qb] + PART * kb:OFF[qb] + PART * kb + PART],
                                         sh.ident[:, :])
            mm.then_inc(t_mm, 1)

        def pe_pv(pe, b, g, kb):
            G = KC * b + g
            P = 2 * G + 1
            if kb == 0:
                pe.wait_ge(pv_out, PO0 + G)
                pe.wait_ge(v_loaded if cross else v_out, (16 if cross else NT) * (b + 1))
            pe.wait_ge(*copied(P, NT + kb))
            for j in range(4):
                col = PART * (g % KC) + HD * j
                mm = nc.tensor.matmul(pv_bank[HD * j:HD * j + HD, PART * kb:T], V[:, kb, col:col + HD],
                                      prob[kb][:, j, :], start=(kb == 0), stop=(kb == NT - 1))
            mm.then_inc(pv_done, 1)

        def pe_qk(pe, b, p, part, rows_before):
            g, half = (p + 4) // 2, p % 2
            G = KC * b + g
            if cross:
                if half == 0 and part == 4:
                    if not first(G, 1):
                        pe.wait_ge(q_lo, G)
                    if not first(PAIRS * b + p, 2):
                        pe.wait_ge(o_out, O0 + KC * b + p // 2 - 1)
                    if g % KC == 0:
                        pe.wait_ge(ln_done, NT * (b + g // KC + 1))
                    for t in range(NT):
                        mm = nc.tensor.transpose(m_bank[0][:, PART * t:PART * t + PART],
                                                 xln[:, t, PART * (g % KC):PART * (g % KC) + PART], sh.ident[:, :])
                    mm.then_inc(q_mm, 1)
                return
            if part == 0:
                if not first(G, 1):
                    pe.wait_ge(k_lo if half else q_lo, G)
                if g % KC == 0 and half == 0:
                    pe.wait_ge(lnt_lo, KC * (b + g // KC + 1))
                if rows_before is not None:
                    pe.wait_ge(*rows_before)
            w = WK if half else WQ
            for n in (2 * part, 2 * part + 1):
                c, term = divmod(n, 3)
                cols = slice(PART * (g % KC), PART * (g % KC) + PART)
                wh, wl, xh, xl = w_hi[:, w, c, cols], w_lo[:, w, c, cols], xT_hi[:, c, :], xT_lo[:, c, :]
                lhs, rhs = ((wl, xh), (wh, xl), (wh, xh))[term]
                mm = nc.tensor.matmul(m_bank[half][:, :], lhs, rhs, start=(n == 0), stop=(n == 11))
            if part == 5:
                mm.then_inc(k_mm if half else q_mm, 1)

        def pe_lnt(pe, b, c):
            if c == 0:
                pe.wait_ge(ln_done, NT * (b + 1))
            if c < 2 and not first(b, 1):
                pe.wait_ge((q_lo, k_lo)[c], KC * b)
            if c >= 2:
                pe.wait_ge(lnt_lo, KC * b + c - 1)
            for t in range(NT):
                mm = nc.tensor.transpose(m_bank[c % 2][:, PART * t:PART * t + PART],
                                         xln[:, t, PART * c:PART * c + PART], sh.ident[:, :])
            mm.then_inc(lnt_mm, 1)

        def pe_row(out, lhs, w, t):
            rows = slice(PART * t, PART * t + PART)
            for c in range(KC):
                mm = mm3(out[:, :], (lhs[0][:, c, rows], lhs[1][:, c, rows]), (w_hi[:, w, c, :], w_lo[:, w, c, :]),
                         c == 0, c == KC - 1)
            return mm

        def pe_v(pe, b, t):
            if t == 0:
                pe.wait_ge(k_lo, KC * b + 2)
            else:
                pe.wait_ge(v_out, NT * b + t)
            pe_row(m_bank[1], (xT_hi, xT_lo), WV, t).then_inc(v_mm, 1)

        def pe_o(pe, b, t, last):
            if t == 0:
                pe.wait_ge(pv_out, PO0 + KC * (b + 1))
                if not last:
                    pe.wait_ge(q_lo, KC * (b + 1) + 3)
            elif not (last and t == 1):
                pe.wait_ge(o_out, O0 + NT * b + t - int(last))
            pe_row(m_bank[t % 2 if last else 0], (cx_hi, cx_lo), WO, t).then_inc(o_mm, 1)

        def pe_back(pe, b, g, q_done):
            G = KC * b + g
            pe.wait_ge(pv_out, PO0 + G + 1)
            pe.wait_ge(o_out, O0 + G)
            pe.wait_ge(q_lo, q_done)
            for t in range(NT):
                mm = nc.tensor.transpose(m_bank[0][:, PART * t:PART * t + PART], cn[:, PART * t:PART * t + PART],
                                         sh.ident[:, :])
            mm.then_inc(o_mm, 1)

        @block.tensor
        def _(pe):
            pe.sem_inc(pv_done, PV0)
            pe.sem_inc(o_mm, O0)

            def step(b, p, s_=True, t_=True, tail=True, qk_=True, v_=False, o_=False, lnt0_=False, lnt_=False, rows_before=None,
                     last=False):
                for i in range(PAIRS):
                    if s_:
                        pe_s(pe, b, p + 1, i)
                    if t_:
                        pe_t(pe, b, p, i)
                    if t_ and p % 2 == 1 and i == 7:
                        pe_pv(pe, b, p // 2, 0)
                    if tail and p % 2 == 0 and i < 3:
                        pe_pv(pe, b, p // 2 - 1, i + 1)
                    if lnt_ and i < KC - 1:
                        pe_lnt(pe, b + 1, i + 1)
                    parts = {5: (0, 1), 6: (2, 3), 7: (4, 5)}.get(i, ()) if lnt_ else (i - 1,)
                    for part in parts:
                        if qk_ and 0 <= part <= 5:
                            pe_qk(pe, b, p, part, rows_before)
                    if lnt0_ and i == 7:
                        pe_lnt(pe, b + 1, 0)
                    if cross and t_ and tail and p % 2 == 1 and i == 3:
                        pe_back(pe, b, (p - 3) // 2, KC * b + min((p + 3) // 2 + 1, KC if last else PAIRS))
                    if v_ and not cross and i % 2 == 1:
                        pe_v(pe, b, i // 2)
                    if o_ and not cross and i % 2 == 1:
                        pe_o(pe, b - 1, i // 2, False)

            if not cross:
                pe.wait_ge(made, 5)
                for c in range(KC):
                    pe_lnt(pe, 0, c)
            for p in range(-4, 0):
                if not cross:
                    pe.wait_ge(w_lo_done, min(p + 5, 3))
                step(0, p, s_=p == -1, t_=False, tail=False)
            step(0, 0, tail=False, v_=True)
            if not cross:
                pe.wait_ge(w_lo_done, 4)
            step(0, 1, tail=False, rows_before=None if cross else (v_out, NT))

            def batch(b, last):
                for p in range(2, PAIRS):
                    step(b, p, s_=p < 7 or not last, qk_=p < 4 or not last, last=last,
                         lnt0_=p == 3 and not cross and not last, lnt_=p == 4 and not cross and not last,
                         rows_before=(o_out, O0 + NT * b) if p == 2 and not cross else None)
                if last:
                    pe_pv(pe, b, KC - 1, 1)
                    pe_pv(pe, b, KC - 1, 2)
                    pe_pv(pe, b, KC - 1, 3)
                    if cross:
                        pe_back(pe, b, KC - 1, KC * B)
                    else:
                        for t in range(NT):
                            pe_o(pe, b, t, True)
                    return
                step(b + 1, 0, v_=True)
                step(b + 1, 1, o_=True, rows_before=None if cross else (v_out, NT * (b + 2)))

            with pe.Fori(0, B - 1) as b:
                batch(b, False)
            batch(B - 1, True)

        def dve_s(dve, b, p, i):
            h, qb = divmod(i, NT)
            n = PAIRS * (PAIRS * b + p) + i
            N = PART * (qb + 1)
            wait_alone(dve, s_mm, n + 1, dve_passed)
            nc.vector.tensor_tensor_reduce(probs[:, p % 2, h, OFF[qb]:OFF[qb + 1]], s_bank[i % NS][:, 0:N],
                                           sh.mask[:, T - N:T], -SCALE, BIG, ALU.add, ALU.min,
                                           negmax[:, p % 2, h, qb:qb + 1]).then_inc(s_max, 1)

        def dve_recip(dve, b, p, h, part):
            dve.wait_ge(p_exp, PAIRS * (PAIRS * b + p) + NT * h + 3 + part)
            qs = slice(3, 4) if part else slice(0, 3)
            nc.vector.reciprocal(rsum[:, p % 2, h, qs], rowsum[:, p % 2, h, qs]).then_inc(r_done, 1)

        def dve_t(dve, b, p, i):
            h, kb = divmod(i, NT)
            P = PAIRS * b + p
            dve.wait_ge(t_mm, PAIRS * P + i + 1)
            if p % 2 == 0 and (h == 0 or i - NT not in T_DVE):
                dve.wait_ge(pv_done, PV0 + NT * (KC * b + p // 2 - 1) + kb + 1)
            nc.vector.tensor_copy(prob[kb][:, 2 * (p % 2) + h, :], t_bank[i % NTB][:, 0:T - PART * kb]).then_inc(t_dve, 1)

        def dve_qk(dve, b, p):
            g, half = (p + 4) // 2, p % 2
            G = KC * b + g
            if cross and half:
                return
            dve.wait_ge(k_hi if half else q_hi, G + 1)
            out = stage[:, g % 2, KL if half else QL, :]
            hi = f32(stage[:, g % 2, KH if half else QH, :])
            if cross:
                nc.vector.tensor_tensor(out, m_bank[0][:, :], hi, ALU.subtract).then_inc(q_lo, 1)
            else:
                nc.vector.scalar_tensor_tensor(out=out, in0=m_bank[half][:, :],
                                               scalar=sh.bias[:, half, g % KC:g % KC + 1],
                                               in1=hi, op0=ALU.add, op1=ALU.subtract)\
                    .then_inc(k_lo if half else q_lo, 1)

        def dve_k(dve, b, p):
            g = (p + 4) // 2
            dve.wait_ge(kraw_in[g % 2], 16 * (2 * b + g // 2 + 1))
            nc.vector.tensor_copy(stage[:, g % 2, KH, :], kraw[:, g % 2, :]).then_inc(k_hi, 1)

        def dve_ln_stats(dve, b, t):
            dve.wait_ge(x_loaded[t], 16 * (b + LN0))
            nc.vector.bn_stats(stats[:, t, :], xt[:, t, :]).then_inc(ln_stat, 1)
            wait_alone(dve, ln_stat, NT * (b + LN0 - 1) + t + 1, dve_passed)
            nc.vector.bn_aggr(mv[:, t, :], stats[:, t, :]).then_inc(ln_mv, 1)

        def dve_ln_norm(dve, b, t):
            if t == 0 and not first(b + LN0, 1):
                dve.wait_ge(ln_rstd, b + LN0)
            nc.vector.tensor_scalar(xln[:, t, :], xt[:, t, :], mv[:, t, 0:1], rstd[:, t:t + 1],
                                    ALU.subtract, ALU.mult).then_inc(ln_done, 1)

        def dve_lnt(dve, b, c):
            dve.wait_ge(lnt_hi, KC * b + c + 1)
            nc.vector.tensor_tensor(xT_lo[:, c, :], m_bank[c % 2][:, :], f32(xT_hi[:, c, :]), ALU.subtract)\
                .then_inc(lnt_lo, 1)

        def dve_cx(dve, b, g):
            G = KC * b + g
            dve.wait_ge(cx_hi_done, G + 1)
            nc.vector.scalar_tensor_tensor(out=cx_lo[:, g % KC, :], in0=pv_bank[:, :],
                                           scalar=sh.bias[:, 2, g % KC:g % KC + 1], in1=f32(cx_hi[:, g % KC, :]),
                                           op0=ALU.add, op1=ALU.subtract).then_inc(pv_out, 1)

        def dve_back(dve, b, g):
            G = KC * b + g
            dve.wait_ge(o_mm, O0 + G + 1)
            if g % KC == 0:
                dve.wait_ge(res_loaded, 16 * (b + 1))
            cols = slice(PART * (g % KC), PART * (g % KC) + PART)
            nc.vector.tensor_tensor(xres[:, :, cols], m_bank[0][:, :].rearrange("p (t n) -> p t n", t=NT),
                                    xres[:, :, cols], ALU.add).then_inc(o_out, 1)

        def dve_o(dve, b, t, last):
            if t == 0:
                dve.wait_ge(res_biased, NT * (b + 1))
            dve.wait_ge(o_mm, O0 + NT * b + t + 1)
            nc.vector.tensor_tensor(xres[:, t, :], m_bank[t % 2 if last else 0][:, :], xres[:, t, :], ALU.add).then_inc(o_out, 1)

        @block.vector
        def _(dve):
            dve.sem_inc(t_dve, TD0)
            dve.sem_inc(o_out, O0)
            if not cross:
                dve.sem_inc(pv_out, PO0)

            def step(b, p, s_=True, t_=True, tail=True, lo_=True, k_=True, o_=False, norm_=True, lnt_=False):
                for i in range(PAIRS):
                    if s_:
                        dve_s(dve, b, p + 1, i)
                    if t_ and i in T_DVE:
                        dve_t(dve, b, p, i)
                    if i == 0:
                        if t_:
                            dve_recip(dve, b, p, 1, 1)
                        if lo_:
                            dve_qk(dve, b, p - 1)
                    if lnt_ and i < KC:
                        dve_lnt(dve, b + 1, i)
                    if (p, i) in STAT_AT:
                        dve_ln_stats(dve, b + 1, STAT_AT[p, i])
                    if p == NORM_STEP and norm_ and 1 <= i <= 4:
                        if cross and i == 1:
                            dve.wait_ge(q_mm, KC * (b + 1))
                        dve_ln_norm(dve, b + 1, i - 1)
                    if s_ and i in (3, 4, 7):
                        h, part = {3: (0, 0), 4: (0, 1), 7: (1, 0)}[i]
                        dve_recip(dve, b, p + 1, h, part)
                    if not cross and tail and p % 2 == 0 and i == 6:
                        dve_cx(dve, b, p // 2 - 1)
                    if cross and k_ and p % 2 == 1 and i == 5:
                        dve_k(dve, b, p)
                    if cross and t_ and tail and p % 2 == 1 and i == 7:
                        dve_back(dve, b, (p - 3) // 2)
                    if o_ and not cross and i % 2 == 1:
                        dve_o(dve, b - 1, i // 2, False)

            if not cross:
                for t in range(NT):
                    dve_ln_stats(dve, 0, t)
            for t in range(NT):
                if cross:
                    nc.vector.tensor_copy(xln[:, t, :], xt[:, t, :]).then_inc(ln_done, 1)
                else:
                    dve_ln_norm(dve, 0, t)
            if not cross:
                dve.wait_ge(made, 5)
                dve.wait_ge(small_in, 64)
                for c in range(KC):
                    dve_lnt(dve, 0, c)
            for p in range(-4, 0):
                step(0, p, s_=p == -1, t_=False, tail=False, lo_=p > -4)
            step(0, 0, tail=False)
            step(0, 1, tail=False)

            def batch(b, last):
                for p in range(2, PAIRS):
                    step(b, p, s_=p < 7 or not last, lo_=p < 5 or not last, lnt_=p == 4 and not cross and not last, k_=p < 4 or not last,
                         norm_=not last)
                if last:
                    if cross:
                        dve_back(dve, b, KC - 1)
                    else:
                        dve_cx(dve, b, KC - 1)
                        for t in range(NT):
                            dve_o(dve, b, t, True)
                    return
                step(b + 1, 0)
                step(b + 1, 1, o_=True)

            with dve.Fori(0, B - 1) as b:
                batch(b, False)
            batch(B - 1, True)

        def act_exp(act, b, p, i):
            h, qb = divmod(i, NT)
            act.wait_ge(s_max, PAIRS * (PAIRS * b + p) + i + 1)
            tile = probs[:, p % 2, h, OFF[qb]:OFF[qb + 1]]
            nc.scalar.activation(tile, tile, ACT.Exp, bias=negmax[:, p % 2, h, qb:qb + 1], scale=-1.0,
                                 accum_out=rowsum[:, p % 2, h, qb:qb + 1]).then_inc(p_exp, 1)

        def act_t(act, b, p, i):
            h, kb = divmod(i, NT)
            P = PAIRS * b + p
            act.wait_ge(t_mm, PAIRS * P + i + 1)
            if p % 2 == 0 and h == 0:
                act.wait_ge(pv_done, PV0 + NT * (KC * b + p // 2 - 1) + kb + 1)
            nc.scalar.activation(prob[kb][:, 2 * (p % 2) + h, :], t_bank[i % NTB][:, 0:T - PART * kb], ACT.Copy)\
                .then_inc(t_act, 1)

        def act_qk(act, b, p):
            g, half = (p + 4) // 2, p % 2
            G = KC * b + g
            out = stage[:, g % 2, KH if half else QH, :]
            if cross and half:
                return
            if cross:
                act.wait_ge(q_mm, G + 1)
                nc.scalar.activation(out, m_bank[0][:, :], ACT.Copy).then_inc(q_hi, 1)
            else:
                act.wait_ge(k_mm if half else q_mm, G + 1)
                nc.scalar.activation(out, m_bank[half][:, :], ACT.Identity, bias=sh.bias[:, half, g % KC:g % KC + 1])\
                    .then_inc(k_hi if half else q_hi, 1)

        def act_lnt(act, b, c):
            act.wait_ge(lnt_mm, KC * b + c + 1)
            nc.scalar.activation(xT_hi[:, c, :], m_bank[c % 2][:, :], ACT.Copy).then_inc(lnt_hi, 1)

        def act_pv(act, b, g):
            G = KC * b + g
            act.wait_ge(pv_done, PV0 + NT * (G + 1))
            if cross:
                act.wait_ge(o_mm, O0 + G)
                nc.scalar.activation(cn[:, :], pv_bank[:, :], ACT.Copy).then_inc(pv_out, 1)
                return
            if g % KC == 0:
                act.wait_ge(o_mm, O0 + NT * b)
            nc.scalar.activation(cx_hi[:, g % KC, :], pv_bank[:, :], ACT.Identity,
                                 bias=sh.bias[:, 2, g % KC:g % KC + 1]).then_inc(cx_hi_done, 1)

        def act_v(act, b, t):
            act.wait_ge(v_mm, NT * b + t + 1)
            act.wait_ge(pv_done, PV0 + NT * (KC * b - 1) + t + 1)
            nc.scalar.activation(V[:, t, :], m_bank[1][:, :], ACT.Copy).then_inc(v_out, 1)

        @block.scalar
        def _(act):
            act.sem_inc(t_act, TA0)
            if cross:
                act.sem_inc(pv_out, PO0)

            def step(b, p, s_=True, t_=True, tail=True, qk_=True, v_=False, lnt0_=False, lnt_=False):
                for i in range(PAIRS):
                    if lnt_ and i < KC - 1:
                        act_lnt(act, b + 1, i + 1)
                    if t_ and i in T_ACT:
                        act_t(act, b, p, i)
                    if s_:
                        act_exp(act, b, p + 1, i)
                    if tail and p % 2 == 0 and i == 4:
                        act_pv(act, b, p // 2 - 1)
                    if v_ and not cross and i % 2 == 1:
                        act_v(act, b, i // 2)
                if qk_:
                    act_qk(act, b, p)
                if lnt0_:
                    act_lnt(act, b + 1, 0)

            def split(i):
                act.wait_ge(w_loaded[i], 16)
                nc.scalar.activation(w_hi[:, i], raw[i], ACT.Copy).then_inc(w_hi_done, 1)

            if not cross:
                split(WQ)
                split(WK)
                for c in range(KC):
                    act_lnt(act, 0, c)
                act.wait_ge(small_in, 64)
                split(WV)
                split(WO)
            for p in range(-4, 0):
                step(0, p, s_=p == -1, t_=False, tail=False)
            step(0, 0, tail=False, v_=True)
            step(0, 1)

            def batch(b, last):
                for p in range(2, PAIRS):
                    step(b, p, s_=p < 7 or not last, qk_=p < 4 or not last, lnt0_=p == 3 and not cross and not last,
                         lnt_=p == 4 and not cross and not last)
                if last:
                    act_pv(act, b, KC - 1)
                    return
                step(b + 1, 0, v_=True)
                step(b + 1, 1)

            with act.Fori(0, B - 1) as b:
                batch(b, False)
            batch(B - 1, True)

        def pool_p(pool, b, p, i):
            h, qb = divmod(i, NT)
            wait_alone(pool, r_done, 2 * (2 * (PAIRS * b + p) + h) + 1 + qb // 3, pool_passed)
            tile = probs[:, p % 2, h, OFF[qb]:OFF[qb + 1]]
            nc.gpsimd.tensor_scalar(tile, tile, rsum[:, p % 2, h, qb:qb + 1], 0.0, ALU.mult, ALU.add)\
                .then_inc(p_done, 1)

        def pool_rstd(pool, b):
            wait_alone(pool, ln_mv, NT * (b + LN0), pool_passed)
            nc.gpsimd.tensor_scalar(veps[:, :], mv[:, :, 1], EPS, None, ALU.add).then_inc(ln_eps, 1)
            pool.wait_ge(ln_eps, b + LN0)
            nc.gpsimd.tensor_tensor(rstd[:, :], veps[:, :], sh.neg_half[:, 0:NT], ALU.pow).then_inc(ln_rstd, 1)

        def pool_k(pool, b, p):
            g = (p + 4) // 2
            pool.wait_ge(k_hi, KC * b + g + 1)
            nc.gpsimd.tensor_tensor(stage[:, g % 2, KL, :], kraw[:, g % 2, :], f32(stage[:, g % 2, KH, :]),
                                    ALU.subtract).then_inc(k_lo, 1)

        def pool_res(pool, b, t):
            if t == 0:
                pool.wait_ge(res_loaded, 16 * (b + 1))
            nc.gpsimd.tensor_tensor(xres[:, t, :], xres[:, t, :], sh.o_bias[:, :], ALU.add).then_inc(res_biased, 1)

        @block.gpsimd
        def _(pool):
            if not cross:
                nc.gpsimd.memset(sh.neg_half[:, :], -0.5).then_inc(made, 1)
                nc.gpsimd.memset(sh.ident[:, :], 0.0).then_inc(made, 1)
                nc.gpsimd.memset(sh.mask[:, :], 0.0).then_inc(made, 1)
                pool.wait_ge(made, 3)
                nc.gpsimd.affine_select(out=sh.ident[:, :], in_=sh.ident[:, :], compare_op=ALU.not_equal, fill=1.0,
                                        base=0, pattern=[[-1, PART]], channel_multiplier=1).then_inc(made, 1)
                own = sh.mask[:, T - PART:T]
                nc.gpsimd.affine_select(out=own, in_=own, compare_op=ALU.is_ge, fill=MASKED, base=0,
                                        pattern=[[-1, PART]], channel_multiplier=1).then_inc(made, 1)
                pool_rstd(pool, 0)
                for i in (WQ, WK, WV, WO):
                    pool.wait_ge(w_hi_done, i + 1)
                    nc.gpsimd.tensor_tensor(w_lo[:, i], raw[i], f32(w_hi[:, i]), ALU.subtract)\
                        .then_inc(w_lo_done, 1)
                pool.wait_ge(small_in, 64)

            def step(b, p, s_=True, t_=True, qk_=True):
                if t_:
                    pool_p(pool, b, p, PAIRS - 1)
                for i in range(PAIRS - 1):
                    if s_:
                        pool_p(pool, b, p + 1, i)
                    if (p, i) == max(STAT_AT):
                        pool_rstd(pool, b + 1)
                if not cross and p >= 4:
                    pool_res(pool, b, p - 4)
                if cross and qk_ and p % 2 == 1:
                    pool_k(pool, b, p)

            for p in range(-4, 0):
                step(0, p, s_=p == -1, t_=False)
            step(0, 0)
            step(0, 1)

            def batch(b, last):
                for p in range(2, PAIRS):
                    step(b, p, s_=p < 7 or not last, qk_=p < 4 or not last)
                if last:
                    return
                step(b + 1, 0)
                step(b + 1, 1)

            with pool.Fori(0, B - 1) as b:
                batch(b, False)
            batch(B - 1, True)


def ffn(nc, sh):
    x_in = sh.dram["x3"].rearrange("(b t p) n -> b p t n", b=B, p=PART)
    x_out = sh.dram["out"].rearrange("(b t p) n -> b p t n", b=B, p=PART)
    w_hi, w_lo = sh.w_hi, sh.w_lo
    UP, EXPERT, DOWN = range(3)
    with ExitStack() as ctx:
        def sb(name, shape, dt=F32):
            return ctx.enter_context(nc.sbuf_tensor(f"f_{name}", shape, dt))

        def sem(name):
            return ctx.enter_context(nc.semaphore(f"f_{name}"))

        xt, stats, mv, veps, rstd = sh.xt, sh.stats, sh.mv, sh.veps, sh.rstd
        xln = sb("xln", [PART, NT, D])
        xres = sh.xres
        xT_hi = sb("xT_hi", [PART, KC, T], F32R)
        xT_lo = sb("xT_lo", [PART, KC, T], F32R)
        h_hi = sb("h_hi", [PART, KC, T], F32R)
        h_lo = sb("h_lo", [PART, KC, T], F32R)
        g_hi = sb("g_hi", [PART, KC, PART], F32R)
        g_lo = sb("g_lo", [PART, KC, PART], F32R)
        lg = sb("lg", [PART, T])
        logits = sb("logits", [PART, NT, NE])
        top = sb("top", [PART, NT, 8])
        gap = sb("gap", [PART, NT])
        e2 = sb("e2", [PART, NT])
        den = sb("den", [PART, NT])
        rw1 = sb("rw1", [PART, NT])
        rw2 = sb("rw2", [PART, NT])
        rw = sb("rw", [PART, NT])
        bank = [ctx.enter_context(nc.psum_tensor(f"f_b{i}", [PART, T], F32)) for i in range(8)]
        T_BANK, UP_BANK, GATE_BANK, DOWN_BANK, EXP_BANK = bank[0], bank[1:3], bank[3], bank[4:6], bank[6:8]

        x_loaded = [sem(f"x_loaded{t}") for t in range(NT)]
        res_loaded, stored = sem("res_loaded"), sem("stored")
        w_hi_done, w_lo_done = sem("w_hi_done"), sem("w_lo_done")
        dve_passed, pool_passed = sem("dve_passed"), sem("pool_passed")
        ln_stat, ln_mv, ln_eps, ln_rstd, ln_done = (sem(n) for n in ("ln_stat", "ln_mv", "ln_eps", "ln_rstd",
                                                                     "ln_done"))
        lnt_mm, lnt_hi, lnt_lo = sem("lnt_mm"), sem("lnt_hi"), sem("lnt_lo")
        up_mm, h_hi_done, h_lo_done = sem("up_mm"), sem("h_hi_done"), sem("h_lo_done")
        cleared = sem("cleared")
        gate_mm, lg_done, gate_t, gate_out = sem("gate_mm"), sem("lg_done"), sem("gate_t"), sem("gate_out")
        g_step = sem("g_step")
        e2_done = sem("e2_done")
        exp_mm, exp_out = sem("exp_mm"), sem("exp_out")
        down_mm, y_done = sem("down_mm"), sem("y_done")
        GSTEPS = NT + 5

        def t_bank(b, c):
            return bank[4 + c] if isinstance(b, int) and b == 0 else T_BANK

        block = ctx.enter_context(nc.Block())

        @block.sync
        def _(sp):
            def load(b):
                for t in range(NT):
                    sp.dma_start(xt[:, t, :], x_in[b][:, t, :]).then_inc(x_loaded[t], 16)

            sp.wait_ge(sh.stored[1], 16 * B)
            sp.dma_start(xres[:, :, :], x_in[0]).then_inc(res_loaded, 16)

            def batch(b, last):
                if not last:
                    sp.wait_ge(ln_done, NT * (b + 1))
                    load(b + 1)
                sp.wait_ge(y_done, NT * (b + 1))
                sp.dma_start(x_out[b], xres[:, :, :]).then_inc(stored, 16)
                sp.wait_ge(stored, 16 * (b + 1))
                if not last:
                    sp.dma_start(xres[:, :, :], x_in[b + 1]).then_inc(res_loaded, 16)

            with sp.Fori(0, B - 1) as b:
                batch(b, False)
            batch(B - 1, True)

        @block.tensor
        def _(pe):
            def three(out, lhs, rhs, first, last):
                nc.tensor.matmul(out, lhs[1], rhs[0], start=first, stop=False)
                nc.tensor.matmul(out, lhs[0], rhs[1], start=False, stop=False)
                return nc.tensor.matmul(out, lhs[0], rhs[0], start=False, stop=last)

            def lnt(b, c):
                if c == 0:
                    pe.wait_ge(ln_done, NT * (b + 1))
                if not (isinstance(b, int) and b == 0):
                    pe.wait_ge(lnt_lo, KC * b + c)
                for t in range(NT):
                    mm = nc.tensor.transpose(t_bank(b, c)[:, PART * t:PART * t + PART],
                                             xln[:, t, PART * c:PART * c + PART], sh.ident[:, :])
                mm.then_inc(lnt_mm, 1)

            for c in range(KC):
                lnt(0, c)

            def batch(b, last):
                pe.wait_ge(lnt_lo, KC * (b + 1))
                pe.wait_ge(w_lo_done, 2)
                for c in range(KC):
                    mm = three(GATE_BANK[:, :], (g_hi[:, c, :], g_lo[:, c, :]), (xT_hi[:, c, :], xT_lo[:, c, :]),
                               c == 0, c == KC - 1)
                mm.then_inc(gate_mm, 1)
                for m in range(KC):
                    if m >= 2:
                        pe.wait_ge(h_lo_done, KC * b + m - 1)
                    for c in range(KC):
                        cols = slice(PART * m, PART * m + PART)
                        mm = three(UP_BANK[m % 2][:, :], (w_hi[:, UP, c, cols], w_lo[:, UP, c, cols]),
                                   (xT_hi[:, c, :], xT_lo[:, c, :]), c == 0, c == KC - 1)
                    mm.then_inc(up_mm, 1)
                    if m == 0:
                        pe.wait_ge(lg_done, b + 1)
                        for t in range(NT):
                            mm = nc.tensor.transpose(GATE_BANK[:, PART * t:PART * t + PART],
                                                     lg[:, PART * t:PART * t + PART], sh.ident[:, :])
                        mm.then_inc(gate_t, 1)
                pe.wait_ge(w_lo_done, 3)
                for t in range(NT):
                    rows = slice(PART * t, PART * t + PART)
                    if t >= 2:
                        pe.wait_ge(exp_out, NT * b + t - 1)
                    for c in range(KC):
                        mm = three(EXP_BANK[t % 2][:, :], (xT_hi[:, c, rows], xT_lo[:, c, rows]),
                                   (w_hi[:, EXPERT, c, :], w_lo[:, EXPERT, c, :]), c == 0, c == KC - 1)
                    mm.then_inc(exp_mm, 1)
                pe.wait_ge(h_lo_done, KC * (b + 1))
                pe.wait_ge(w_lo_done, 4)
                for t in range(NT):
                    rows = slice(PART * t, PART * t + PART)
                    if not last:
                        lnt(b + 1, t)
                    if t >= 2:
                        pe.wait_ge(y_done, NT * b + t - 1)
                    for c in range(KC):
                        mm = three(DOWN_BANK[t % 2][:, :], (h_hi[:, c, rows], h_lo[:, c, rows]),
                                   (w_hi[:, DOWN, c, :], w_lo[:, DOWN, c, :]), c == 0, c == KC - 1)
                    mm.then_inc(down_mm, 1)

            with pe.Fori(0, B - 1) as b:
                batch(b, False)
            batch(B - 1, True)

        @block.vector
        def _(dve):
            def ln_stats(b, t):
                dve.wait_ge(x_loaded[t], 16 * b)
                nc.vector.bn_stats(stats[:, t, :], xt[:, t, :]).then_inc(ln_stat, 1)
                wait_alone(dve, ln_stat, NT * (b - 1) + t + 1, dve_passed)
                nc.vector.bn_aggr(mv[:, t, :], stats[:, t, :]).then_inc(ln_mv, 1)

            def ln_norm(b, t):
                if t == 0 and not (isinstance(b, int) and b == 0):
                    dve.wait_ge(ln_rstd, b)
                nc.vector.tensor_scalar(xln[:, t, :], xt[:, t, :], mv[:, t, 0:1], rstd[:, t:t + 1],
                                        ALU.subtract, ALU.mult).then_inc(ln_done, 1)

            def lnt(b, c):
                dve.wait_ge(lnt_hi, KC * b + c + 1)
                nc.vector.tensor_tensor(xT_lo[:, c, :], t_bank(b, c)[:, :], f32(xT_hi[:, c, :]), ALU.subtract)\
                    .then_inc(lnt_lo, 1)

            for t in range(NT):
                ln_norm(0, t)
            for c in range(KC):
                lnt(0, c)

            def batch(b, last):
                done = GSTEPS * b
                for m in range(KC):
                    if not last:
                        ln_stats(b + 1, m)
                    dve.wait_ge(h_hi_done, KC * b + m + 1)
                    nc.vector.scalar_tensor_tensor(out=h_lo[:, m, :], in0=UP_BANK[m % 2][:, :], scalar=0.0,
                                                   in1=f32(h_hi[:, m, :]), op0=ALU.max, op1=ALU.subtract)\
                        .then_inc(h_lo_done, 1)
                    if m == 0:
                        dve.wait_ge(gate_t, b + 1)
                        nc.vector.tensor_copy(logits[:, :, :],
                                              GATE_BANK[:, :].rearrange("p (t e) -> p t e", t=NT)[:, :, 0:NE])\
                            .then_inc(gate_out, 1)
                        wait_alone(dve, gate_out, b + 1, dve_passed)
                        for t in range(NT):
                            nc.vector.max(top[:, t, :], logits[:, t, :]).then_inc(g_step, 1)
                        dve.wait_ge(g_step, done + NT)
                        nc.vector.tensor_tensor(gap[:, :], top[:, :, 1], top[:, :, 0], ALU.subtract)\
                            .then_inc(g_step, 1)
                dve.wait_ge(e2_done, b + 1)
                nc.vector.tensor_scalar(den[:, :], e2[:, :], 1.0, None, ALU.add).then_inc(g_step, 1)
                dve.wait_ge(g_step, done + NT + 2)
                nc.vector.reciprocal(rw1[:, :], den[:, :]).then_inc(g_step, 1)
                dve.wait_ge(g_step, done + NT + 3)
                nc.vector.tensor_tensor(rw2[:, :], e2[:, :], rw1[:, :], ALU.mult).then_inc(g_step, 1)
                dve.wait_ge(g_step, done + NT + 4)
                nc.vector.tensor_tensor(rw[:, :], rw1[:, :], rw2[:, :], ALU.add).then_inc(g_step, 1)
                dve.wait_ge(g_step, done + NT + 5)
                dve.wait_ge(res_loaded, 16 * (b + 1))
                for t in range(NT):
                    if not last:
                        ln_norm(b + 1, t)
                    dve.wait_ge(exp_mm, NT * b + t + 1)
                    nc.vector.scalar_tensor_tensor(out=xres[:, t, :], in0=EXP_BANK[t % 2][:, :],
                                                   scalar=rw[:, t:t + 1], in1=xres[:, t, :], op0=ALU.mult,
                                                   op1=ALU.add).then_inc(exp_out, 1)
                dve.wait_ge(exp_out, NT * (b + 1))
                for t in range(NT):
                    if not last:
                        lnt(b + 1, t)
                    dve.wait_ge(down_mm, NT * b + t + 1)
                    nc.vector.tensor_tensor(xres[:, t, :], DOWN_BANK[t % 2][:, :], xres[:, t, :], ALU.add)\
                        .then_inc(y_done, 1)

            with dve.Fori(0, B - 1) as b:
                batch(b, False)
            batch(B - 1, True)

        @block.scalar
        def _(act):
            act.wait_ge(cleared, 2)
            nc.scalar.activation(g_hi[:, :, 0:NE], sh.g_raw[:, :, :], ACT.Copy).then_inc(w_hi_done, 1)
            for s in (UP, EXPERT, DOWN):
                nc.scalar.activation(w_hi[:, s], sh.ffn_raw[:, s], ACT.Copy).then_inc(w_hi_done, 1)

            def lnt(b, c):
                act.wait_ge(lnt_mm, KC * b + c + 1)
                nc.scalar.activation(xT_hi[:, c, :], t_bank(b, c)[:, :], ACT.Copy).then_inc(lnt_hi, 1)

            for c in range(KC):
                lnt(0, c)

            def batch(b, last):
                act.wait_ge(gate_mm, b + 1)
                nc.scalar.activation(lg[:, :], GATE_BANK[:, :], ACT.Copy).then_inc(lg_done, 1)
                for m in range(KC):
                    act.wait_ge(up_mm, KC * b + m + 1)
                    nc.scalar.activation(h_hi[:, m, :], UP_BANK[m % 2][:, :], ACT.Relu).then_inc(h_hi_done, 1)
                    if m == 1:
                        act.wait_ge(g_step, GSTEPS * b + NT + 1)
                        nc.scalar.activation(e2[:, :], gap[:, :], ACT.Exp).then_inc(e2_done, 1)
                if not last:
                    for c in range(KC):
                        lnt(b + 1, c)

            with act.Fori(0, B - 1) as b:
                batch(b, False)
            batch(B - 1, True)

        @block.gpsimd
        def _(pool):
            def norm_factor(b):
                wait_alone(pool, ln_mv, NT * b, pool_passed)
                nc.gpsimd.tensor_scalar(veps[:, :], mv[:, :, 1], EPS, None, ALU.add).then_inc(ln_eps, 1)
                pool.wait_ge(ln_eps, b)
                nc.gpsimd.tensor_tensor(rstd[:, :], veps[:, :], sh.neg_half[:, 0:NT], ALU.pow).then_inc(ln_rstd, 1)

            def lo(n, out, raw, hi):
                pool.wait_ge(w_hi_done, n)
                nc.gpsimd.tensor_tensor(out, raw, f32(hi), ALU.subtract).then_inc(w_lo_done, 1)

            nc.gpsimd.memset(f32(g_hi[:, :, :]), 0.0).then_inc(cleared, 1)
            nc.gpsimd.memset(f32(g_lo[:, :, :]), 0.0).then_inc(cleared, 1)
            lo(1, g_lo[:, :, 0:NE], sh.g_raw[:, :, :], g_hi[:, :, 0:NE])
            lo(2, w_lo[:, UP], sh.ffn_raw[:, UP], w_hi[:, UP])
            lo(3, w_lo[:, EXPERT], sh.ffn_raw[:, EXPERT], w_hi[:, EXPERT])
            lo(4, w_lo[:, DOWN], sh.ffn_raw[:, DOWN], w_hi[:, DOWN])
            with pool.Fori(1, B) as b:
                norm_factor(b)


def decoder_block(nc, dram):
    sh = Shared()
    sh.dram = dram
    with ExitStack() as ctx:
        def sb(name, shape, dt=F32):
            return ctx.enter_context(nc.sbuf_tensor(name, shape, dt))

        sh.w_hi = sb("w_hi", [PART, 4, KC, D], F32R)
        sh.w_lo = sb("w_lo", [PART, 4, KC, D], F32R)
        sh.g_raw = sb("g_raw", [PART, KC, NE])
        sh.ident = sb("ident", [PART, PART])
        sh.neg_half = sb("neg_half", [PART, NT])
        sh.mask = sb("mask", [PART, T])
        sh.xt = sb("xt", [PART, NT, D])
        sh.xres = sb("xres", [PART, NT, D])
        sh.stored = [ctx.enter_context(nc.semaphore(n)) for n in ("self_stored", "cross_stored")]
        sh.stats = sb("stats", [PART, NT, 6])
        sh.mv = sb("mv", [PART, NT, 2])
        sh.veps = sb("veps", [PART, NT])
        sh.rstd = sb("rstd", [PART, NT])
        sh.bias = sb("bias", [PART, 3, KC])
        sh.o_bias = sb("o_bias", [PART, D])

        attention(nc, sh, cross=False)
        sh.ffn_raw = sb("ffn_raw", [PART, 3, KC, D])
        attention(nc, sh, cross=True)
        ffn(nc, sh)


def kernel(**inputs):
    import numpy as _np
    import concourse.bacc as _bacc
    from concourse.bass_utils import run_bass_kernel_spmd as _run

    nc = _bacc.Bacc("TRN2", target_bir_lowering=False, num_devices=1)
    a = {k: _np.asarray(v) for k, v in inputs.items()}
    rows = B * T

    def column(v):
        return v.reshape(KC, PART).T

    laid = {
        "x": a["x"].reshape(rows, D),
        "ctx": a["ctx_2048"].reshape(rows, D),
        "ctxT": a["ctx_2048"].transpose(0, 2, 1).reshape(B * D, T),
        "qT": a["L0_attn_q_w"].T, "kT": a["L0_attn_k_w"].T, "vT": a["L0_attn_v_w"].T, "oT": a["L0_attn_o_w"].T,
        "q_b": column(a["L0_attn_q_b"]), "k_b": column(a["L0_attn_k_b"]),
        "v_b": column(a["L0_attn_v_b"]), "o_b": a["L0_attn_o_b"].reshape(1, D),
        "upT": a["L0_ffn_W_up"].T, "downT": a["L0_ffn_W_down"].T, "expert": a["L0_ffn_W_expert"],
        "gT": a["L0_ffn_W_gate"].T,
    }
    laid = {k: _np.ascontiguousarray(v) for k, v in laid.items()}
    dram = {k: nc.dram_tensor(f"in_{k}", list(v.shape), F32, kind="ExternalInput").ap() for k, v in laid.items()}
    dram["x2"] = nc.dram_tensor("x2", [rows, D], F32, kind="Internal").ap()
    dram["x3"] = nc.dram_tensor("x3", [rows, D], F32, kind="Internal").ap()
    dram["out"] = nc.dram_tensor("out", [rows, D], F32, kind="ExternalOutput").ap()
    decoder_block(nc, dram)
    r = _run(nc, [{f"in_{k}": v for k, v in laid.items()}], core_ids=[0])
    return r.results[0]["out"].reshape(B, T, D)
```
